# Optimizing a Trainium2 kernel written in Bass

```python
import numpy as np
import jax
import jax.numpy as jnp

def _softmax(x, axis=-1):
    return jax.nn.softmax(x, axis=axis)

def _gelu(x):
    return jax.nn.gelu(x, approximate=True)

def _silu(x):
    return jax.nn.silu(x)

def _sigmoid(x):
    return jax.nn.sigmoid(x)

def _layernorm(x, axis=-1, eps=1e-05):
    m = jnp.mean(x, axis=axis, keepdims=True)
    v = jnp.var(x, axis=axis, keepdims=True)
    return (x - m) / jnp.sqrt(v + eps)

def _scatter_add(tgt, idx, src, axis=0):
    return tgt.at[idx].add(src)

def _segment_sum(src, seg, n):
    return jax.ops.segment_sum(src, seg, n)
kernel_name = 'mk_xattn_seq_d2_seqx_r4_07677a'

def setup_inputs(seed: int=0):
    np.random.seed(seed)
    _w = jnp.asarray

    def _rec_inputs():
        import jax
        import jax.numpy as jnp
        _rk = jax.random.key(seed)
        x = 7.22e-05 + 1 * jax.random.normal(jax.random.fold_in(_rk, 1), (64, 128, 256), jnp.float32)
        _lenS = 128 - jax.random.randint(jax.random.fold_in(_rk, 7), (64,), 0, max(1, 128 // 4) + 1, jnp.int32)
        _lenS2 = 128 - jax.random.randint(jax.random.fold_in(_rk, 8), (64,), 0, max(1, 128 // 4) + 1, jnp.int32)
        _ctx_1024P = jax.random.normal(jax.random.fold_in(_rk, 11), (64, 16, 256), jnp.float32)
        _ctx_1024c = jax.random.dirichlet(jax.random.fold_in(_rk, 511), 0.3 * jnp.ones((16,), jnp.float32), (64, 128))
        _ctx_1024t = jnp.einsum('bsk,bkd->bsd', _ctx_1024c, _ctx_1024P)
        _ctx_1024t = _ctx_1024t * jax.lax.rsqrt(jnp.mean(jnp.square(_ctx_1024t)) + 1e-12) * 0.953939
        ctx_1024 = 4.13588e-05 + 0.999923 * (_ctx_1024t + 0.3 * jax.random.normal(jax.random.fold_in(_rk, 611), (64, 128, 256), jnp.float32))
        _validS = jnp.arange(128)[None, :] < _lenS[:, None]
        _validS2 = jnp.arange(128)[None, :] < _lenS2[:, None]
        _causal = jnp.tril(jnp.ones((128, 128), dtype=bool))
        mask_BxS2_ff1 = jnp.where(jnp.ones((64, 128), dtype=bool), 1.0, 0.0).astype(jnp.float32)
        return (x, ctx_1024, mask_BxS2_ff1)
    x, ctx_1024, mask_BxS2_ff1 = _rec_inputs()

    def _L0_xattn_setup():
        import jax, jax.numpy as jnp
        import numpy as np
        import math
        NEG = -1e+32
        B, S, D, H, DFF, L = (16, 128, 256, 8, 1024, 3)
        DK = D // H

        def layernorm(x, g, b, eps=1e-05):
            mu = x.mean(-1, keepdims=True)
            var = ((x - mu) ** 2).mean(-1, keepdims=True)
            return (x - mu) / jnp.sqrt(var + eps) * g + b

        def gen_dam(alphas, E, bmask):
            Hh, Ss, _ = alphas.shape
            g = -jnp.log(E + 1e-05)
            y_soft = jax.nn.softmax(alphas + g, axis=-1)
            idx = jnp.argmax(y_soft, axis=-1)
            y_hard = jax.nn.one_hot(idx, 2, dtype=y_soft.dtype)
            m = y_hard - jax.lax.stop_gradient(y_soft) + y_soft
            m = jnp.broadcast_to(m[:, :, 0:1], (Hh, Ss, Ss))
            m = jnp.triu(m)
            m = jnp.rot90(m, 1, axes=(1, 2))
            i = jnp.arange(Ss)[:, None]
            j = jnp.arange(Ss)[None, :]
            src = jnp.clip(j - i, 0, Ss - 1)
            shifted = m[:, jnp.arange(Ss)[:, None], src]
            mask_tri = jnp.where(j >= i, shifted, 0.0)
            masks = mask_tri + jnp.swapaxes(jnp.triu(mask_tri, 1), 1, 2)
            masks = jnp.triu(masks, bmask)
            return masks

        def attention(q, k, v, src_mask, dam, zero_pad, gammas):
            dk = q.shape[-1]
            Ss = q.shape[2]
            scores = jnp.einsum('bhqd,bhkd->bhqk', q, k) / math.sqrt(dk)
            damb = dam[None]
            smb = src_mask[None, None]
            sc = jnp.where(damb, scores, NEG)
            sc = jax.nn.softmax(sc, axis=-1)
            sc = sc * smb.astype(sc.dtype) * damb.astype(sc.dtype)
            distcum = jnp.cumsum(sc, axis=-1)
            disttot = jnp.sum(sc, axis=-1, keepdims=True)
            pos = jnp.abs(jnp.arange(Ss)[None, :] - jnp.arange(Ss)[:, None]).astype(scores.dtype)
            dist = jnp.sqrt(jnp.clip((disttot - distcum) * pos[None, None], 0.0, None))
            dist = jax.lax.stop_gradient(dist)
            gamma = -jax.nn.softplus(gammas)[None]
            te = jnp.clip(jnp.exp(dist * gamma), 1e-05, 100000.0)
            scores = scores * te
            scores = jnp.where(smb, scores, NEG)
            scores = jnp.where(damb, scores, NEG)
            scores = jax.nn.softmax(scores, axis=-1)
            if zero_pad:
                scores = scores.at[:, :, 0, :].set(0.0)
            return jnp.einsum('bhqk,bhkd->bhqd', scores, v)

        def transformer_layer(bmask, query, key, values, apply_pos, p):
            Bb, Ss, Dd = query.shape
            Hh = p['gammas'].shape[0]
            dam = gen_dam(p['alphas'], p['E'], bmask) == 0
            src_mask = jnp.triu(jnp.ones((Ss, Ss), jnp.int32), bmask) == 0
            k = (key @ p['kW'].T + p['kb']).reshape(Bb, Ss, Hh, -1).transpose(0, 2, 1, 3)
            q = (query @ p['kW'].T + p['kb']).reshape(Bb, Ss, Hh, -1).transpose(0, 2, 1, 3)
            v = (values @ p['vW'].T + p['vb']).reshape(Bb, Ss, Hh, -1).transpose(0, 2, 1, 3)
            att = attention(q, k, v, src_mask, dam, bmask == 0, p['gammas'])
            concat = att.transpose(0, 2, 1, 3).reshape(Bb, Ss, Dd)
            q2 = concat @ p['oW'].T + p['ob']
            x = layernorm(query + q2, p['ln1_g'], p['ln1_b'])
            if apply_pos:
                ff = jax.nn.relu(x @ p['w1'].T + p['b1']) @ p['w2'].T + p['b2']
                x = layernorm(x + ff, p['ln2_g'], p['ln2_b'])
            return x
        key = jax.random.key(seed)
        ks = jax.random.split(key, 16)
        sc = 0.02
        return {'q_embed_data': jax.random.normal(ks[0], (B, S, D), jnp.float32), 'qa_embed_data': jax.random.normal(ks[1], (B, S, D), jnp.float32), 'kW': sc * jax.random.normal(ks[2], (L, D, D), jnp.float32), 'kb': jnp.zeros((L, D), jnp.float32), 'vW': sc * jax.random.normal(ks[3], (L, D, D), jnp.float32), 'vb': jnp.zeros((L, D), jnp.float32), 'oW': sc * jax.random.normal(ks[4], (L, D, D), jnp.float32), 'ob': jnp.zeros((L, D), jnp.float32), 'gammas': 0.5 * jax.random.normal(ks[5], (L, H, 1, 1), jnp.float32), 'alphas': 0.001 * jax.random.normal(ks[6], (L, H, S, 2), jnp.float32), 'ln1_g': jnp.ones((L, D), jnp.float32), 'ln1_b': jnp.zeros((L, D), jnp.float32), 'w1': sc * jax.random.normal(ks[7], (L, DFF, D), jnp.float32), 'b1': jnp.zeros((L, DFF), jnp.float32), 'w2': sc * jax.random.normal(ks[8], (L, D, DFF), jnp.float32), 'b2': jnp.zeros((L, D), jnp.float32), 'ln2_g': jnp.ones((L, D), jnp.float32), 'ln2_b': jnp.zeros((L, D), jnp.float32), 'gumbel_E': jax.random.exponential(ks[9], (L, H, S, 2), jnp.float32)}
    _L0_xattn_all = _L0_xattn_setup()
    _L0_xattn_in = {k: v for k, v in _L0_xattn_all.items() if k in ('kW', 'kb', 'vW', 'vb', 'oW', 'ob', 'gammas', 'alphas', 'ln1_g', 'ln1_b', 'w1', 'b1', 'w2', 'b2', 'ln2_g', 'ln2_b', 'gumbel_E')}
    del _L0_xattn_all

    def _L1_xattn_setup():
        import jax, jax.numpy as jnp
        import numpy as np
        NUM_HEADS = 16
        EMBED_DIM = 256
        HEAD_DIM = EMBED_DIM // NUM_HEADS
        N_LAYERS = 12
        B, TQ, TK = (2, 512, 512)

        def _layer_norm(x, gamma, beta, eps=1e-05):
            mean = jnp.mean(x, axis=-1, keepdims=True)
            var = jnp.var(x, axis=-1, keepdims=True)
            return (x - mean) * jax.lax.rsqrt(var + eps) * gamma + beta
        key = jax.random.key(seed)
        ks = jax.random.split(key, 8)
        target = jax.random.normal(ks[0], (B, TQ, EMBED_DIM), dtype=jnp.float32)
        context = jax.random.normal(ks[1], (B, TK, EMBED_DIM), dtype=jnp.float32)
        pad_mask = jnp.ones((B, TK), dtype=jnp.float32)
        std = 0.02
        wq = std * jax.random.normal(ks[2], (EMBED_DIM, EMBED_DIM), dtype=jnp.float32)
        wk = std * jax.random.normal(ks[3], (EMBED_DIM, EMBED_DIM), dtype=jnp.float32)
        wv = std * jax.random.normal(ks[4], (EMBED_DIM, EMBED_DIM), dtype=jnp.float32)
        proj_std = 0.02 / np.sqrt(2.0 * N_LAYERS)
        wo = proj_std * jax.random.normal(ks[5], (EMBED_DIM, EMBED_DIM), dtype=jnp.float32)
        bo = jnp.zeros((EMBED_DIM,), dtype=jnp.float32)
        ln_gamma = jnp.ones((EMBED_DIM,), dtype=jnp.float32)
        ln_beta = jnp.zeros((EMBED_DIM,), dtype=jnp.float32)
        return {'target': target, 'context': context, 'pad_mask': pad_mask, 'wq': wq, 'wk': wk, 'wv': wv, 'wo': wo, 'bo': bo, 'ln_gamma': ln_gamma, 'ln_beta': ln_beta}
    _L1_xattn_all = _L1_xattn_setup()
    _L1_xattn_in = {k: v for k, v in _L1_xattn_all.items() if k in ('wq', 'wk', 'wv', 'wo', 'bo', 'ln_gamma', 'ln_beta')}
    del _L1_xattn_all
    return {'x': x, 'ctx_1024': ctx_1024, 'mask_BxS2_ff1': mask_BxS2_ff1, 'L0_xattn_kW': _L0_xattn_in['kW'], 'L0_xattn_kb': _L0_xattn_in['kb'], 'L0_xattn_vW': _L0_xattn_in['vW'], 'L0_xattn_vb': _L0_xattn_in['vb'], 'L0_xattn_oW': _L0_xattn_in['oW'], 'L0_xattn_ob': _L0_xattn_in['ob'], 'L0_xattn_gammas': _L0_xattn_in['gammas'], 'L0_xattn_alphas': _L0_xattn_in['alphas'], 'L0_xattn_ln1_g': _L0_xattn_in['ln1_g'], 'L0_xattn_ln1_b': _L0_xattn_in['ln1_b'], 'L0_xattn_w1': _L0_xattn_in['w1'], 'L0_xattn_b1': _L0_xattn_in['b1'], 'L0_xattn_w2': _L0_xattn_in['w2'], 'L0_xattn_b2': _L0_xattn_in['b2'], 'L0_xattn_ln2_g': _L0_xattn_in['ln2_g'], 'L0_xattn_ln2_b': _L0_xattn_in['ln2_b'], 'L0_xattn_gumbel_E': _L0_xattn_in['gumbel_E'], 'L1_xattn_wq': _L1_xattn_in['wq'], 'L1_xattn_wk': _L1_xattn_in['wk'], 'L1_xattn_wv': _L1_xattn_in['wv'], 'L1_xattn_wo': _L1_xattn_in['wo'], 'L1_xattn_bo': _L1_xattn_in['bo'], 'L1_xattn_ln_gamma': _L1_xattn_in['ln_gamma'], 'L1_xattn_ln_beta': _L1_xattn_in['ln_beta']}

def reference(x, ctx_1024, mask_BxS2_ff1, L0_xattn_kW, L0_xattn_kb, L0_xattn_vW, L0_xattn_vb, L0_xattn_oW, L0_xattn_ob, L0_xattn_gammas, L0_xattn_alphas, L0_xattn_ln1_g, L0_xattn_ln1_b, L0_xattn_w1, L0_xattn_b1, L0_xattn_w2, L0_xattn_b2, L0_xattn_ln2_g, L0_xattn_ln2_b, L0_xattn_gumbel_E, L1_xattn_wq, L1_xattn_wk, L1_xattn_wv, L1_xattn_wo, L1_xattn_bo, L1_xattn_ln_gamma, L1_xattn_ln_beta):
    import jax
    import jax.numpy as jnp

    def _L0_xattn_ref(q_embed_data, qa_embed_data, kW, kb, vW, vb, oW, ob, gammas, alphas, ln1_g, ln1_b, w1, b1, w2, b2, ln2_g, ln2_b, gumbel_E):
        import jax, jax.numpy as jnp
        import numpy as np
        import math
        NEG = -1e+32
        B, S, D, H, DFF, L = (16, 128, 256, 8, 1024, 3)
        DK = D // H

        def layernorm(x, g, b, eps=1e-05):
            mu = x.mean(-1, keepdims=True)
            var = ((x - mu) ** 2).mean(-1, keepdims=True)
            return (x - mu) / jnp.sqrt(var + eps) * g + b

        def gen_dam(alphas, E, bmask):
            Hh, Ss, _ = alphas.shape
            g = -jnp.log(E + 1e-05)
            y_soft = jax.nn.softmax(alphas + g, axis=-1)
            idx = jnp.argmax(y_soft, axis=-1)
            y_hard = jax.nn.one_hot(idx, 2, dtype=y_soft.dtype)
            m = y_hard - jax.lax.stop_gradient(y_soft) + y_soft
            m = jnp.broadcast_to(m[:, :, 0:1], (Hh, Ss, Ss))
            m = jnp.triu(m)
            m = jnp.rot90(m, 1, axes=(1, 2))
            i = jnp.arange(Ss)[:, None]
            j = jnp.arange(Ss)[None, :]
            src = jnp.clip(j - i, 0, Ss - 1)
            shifted = m[:, jnp.arange(Ss)[:, None], src]
            mask_tri = jnp.where(j >= i, shifted, 0.0)
            masks = mask_tri + jnp.swapaxes(jnp.triu(mask_tri, 1), 1, 2)
            masks = jnp.triu(masks, bmask)
            return masks

        def attention(q, k, v, src_mask, dam, zero_pad, gammas):
            dk = q.shape[-1]
            Ss = q.shape[2]
            scores = jnp.einsum('bhqd,bhkd->bhqk', q, k) / math.sqrt(dk)
            damb = dam[None]
            smb = src_mask[None, None]
            sc = jnp.where(damb, scores, NEG)
            sc = jax.nn.softmax(sc, axis=-1)
            sc = sc * smb.astype(sc.dtype) * damb.astype(sc.dtype)
            distcum = jnp.cumsum(sc, axis=-1)
            disttot = jnp.sum(sc, axis=-1, keepdims=True)
            pos = jnp.abs(jnp.arange(Ss)[None, :] - jnp.arange(Ss)[:, None]).astype(scores.dtype)
            dist = jnp.sqrt(jnp.clip((disttot - distcum) * pos[None, None], 0.0, None))
            dist = jax.lax.stop_gradient(dist)
            gamma = -jax.nn.softplus(gammas)[None]
            te = jnp.clip(jnp.exp(dist * gamma), 1e-05, 100000.0)
            scores = scores * te
            scores = jnp.where(smb, scores, NEG)
            scores = jnp.where(damb, scores, NEG)
            scores = jax.nn.softmax(scores, axis=-1)
            if zero_pad:
                scores = scores.at[:, :, 0, :].set(0.0)
            return jnp.einsum('bhqk,bhkd->bhqd', scores, v)

        def transformer_layer(bmask, query, key, values, apply_pos, p):
            Bb, Ss, Dd = query.shape
            Hh = p['gammas'].shape[0]
            dam = gen_dam(p['alphas'], p['E'], bmask) == 0
            src_mask = jnp.triu(jnp.ones((Ss, Ss), jnp.int32), bmask) == 0
            k = (key @ p['kW'].T + p['kb']).reshape(Bb, Ss, Hh, -1).transpose(0, 2, 1, 3)
            q = (query @ p['kW'].T + p['kb']).reshape(Bb, Ss, Hh, -1).transpose(0, 2, 1, 3)
            v = (values @ p['vW'].T + p['vb']).reshape(Bb, Ss, Hh, -1).transpose(0, 2, 1, 3)
            att = attention(q, k, v, src_mask, dam, bmask == 0, p['gammas'])
            concat = att.transpose(0, 2, 1, 3).reshape(Bb, Ss, Dd)
            q2 = concat @ p['oW'].T + p['ob']
            x = layernorm(query + q2, p['ln1_g'], p['ln1_b'])
            if apply_pos:
                ff = jax.nn.relu(x @ p['w1'].T + p['b1']) @ p['w2'].T + p['b2']
                x = layernorm(x + ff, p['ln2_g'], p['ln2_b'])
            return x

        def P(l):
            return {'kW': kW[l], 'kb': kb[l], 'vW': vW[l], 'vb': vb[l], 'oW': oW[l], 'ob': ob[l], 'gammas': gammas[l], 'alphas': alphas[l], 'ln1_g': ln1_g[l], 'ln1_b': ln1_b[l], 'w1': w1[l], 'b1': b1[l], 'w2': w2[l], 'b2': b2[l], 'ln2_g': ln2_g[l], 'ln2_b': ln2_b[l], 'E': gumbel_E[l]}
        y = transformer_layer(1, qa_embed_data, qa_embed_data, qa_embed_data, True, P(0))
        x = transformer_layer(1, q_embed_data, q_embed_data, q_embed_data, False, P(1))
        x = transformer_layer(0, x, x, y, True, P(2))
        return x

    def _L1_xattn_ref(target, context, pad_mask, wq, wk, wv, wo, bo, ln_gamma, ln_beta):
        import jax, jax.numpy as jnp
        import numpy as np
        NUM_HEADS = 16
        EMBED_DIM = 256
        HEAD_DIM = EMBED_DIM // NUM_HEADS
        N_LAYERS = 12
        B, TQ, TK = (2, 512, 512)

        def _layer_norm(x, gamma, beta, eps=1e-05):
            mean = jnp.mean(x, axis=-1, keepdims=True)
            var = jnp.var(x, axis=-1, keepdims=True)
            return (x - mean) * jax.lax.rsqrt(var + eps) * gamma + beta
        b, tq, d = target.shape
        tk = context.shape[1]
        resid = target
        q = (target @ wq).reshape(b, tq, NUM_HEADS, HEAD_DIM)
        k = (context @ wk).reshape(b, tk, NUM_HEADS, HEAD_DIM)
        v = (context @ wv).reshape(b, tk, NUM_HEADS, HEAD_DIM)
        scores = jnp.einsum('bqhd,bkhd->bhqk', q, k) * (1.0 / np.sqrt(HEAD_DIM))
        m = pad_mask[:, None, None, :]
        scores = scores * m - (1.0 - m) * jnp.asarray(10000000000.0, scores.dtype)
        attn = jax.nn.softmax(scores, axis=-1)
        out = jnp.einsum('bhqk,bkhd->bqhd', attn, v).reshape(b, tq, d)
        out = out @ wo + bo
        return _layer_norm(out + resid, ln_gamma, ln_beta)
    x = _L0_xattn_ref(x, ctx_1024, L0_xattn_kW, L0_xattn_kb, L0_xattn_vW, L0_xattn_vb, L0_xattn_oW, L0_xattn_ob, L0_xattn_gammas, L0_xattn_alphas, L0_xattn_ln1_g, L0_xattn_ln1_b, L0_xattn_w1, L0_xattn_b1, L0_xattn_w2, L0_xattn_b2, L0_xattn_ln2_g, L0_xattn_ln2_b, L0_xattn_gumbel_E)
    x = _L1_xattn_ref(x, ctx_1024, mask_BxS2_ff1, L1_xattn_wq, L1_xattn_wk, L1_xattn_wv, L1_xattn_wo, L1_xattn_bo, L1_xattn_ln_gamma, L1_xattn_ln_beta)
    return x

_drawn_inputs = setup_inputs


def setup_inputs(seed=0):
    import zlib

    import numpy as np

    out = dict(_drawn_inputs(seed))
    spreads = {'L0_xattn_kb': (0.0, 0.8),
     'L0_xattn_vb': (0.0, 0.1),
     'L0_xattn_ob': (0.0, 0.1),
     'L0_xattn_ln1_g': (1.0, 0.2),
     'L0_xattn_ln1_b': (0.0, 0.1),
     'L0_xattn_b1': (0.0, 0.1),
     'L0_xattn_b2': (0.0, 0.1),
     'L0_xattn_ln2_g': (1.0, 0.2),
     'L0_xattn_ln2_b': (0.0, 0.1),
     'L1_xattn_bo': (0.0, 0.1),
     'L1_xattn_ln_gamma': (1.0, 0.2),
     'L1_xattn_ln_beta': (0.0, 0.1)}
    factors = {'L0_xattn_kW': 8.0,
     'L0_xattn_gammas': 8.0,
     'L0_xattn_gumbel_E': 8.0,
     'L1_xattn_wq': 8.0,
     'L1_xattn_wk': 8.0,
     'L1_xattn_wv': 5.721,
     'L1_xattn_wo': 5.761}
    for name, (base, spread) in spreads.items():
        noise = np.random.default_rng([zlib.crc32(name.encode()), seed]).standard_normal(out[name].shape)
        drawn = base * np.exp(spread * noise) if base else spread * noise
        out[name] = jnp.asarray(drawn.astype(out[name].dtype))
    for name, factor in factors.items():
        out[name] = (out[name] * factor).astype(out[name].dtype)
    return out
```

```python
from contextlib import ExitStack

import concourse.bass as bass
from concourse import mybir

F32 = mybir.dt.float32
BF16 = mybir.dt.bfloat16
I32 = mybir.dt.int32
ALU = mybir.AluOpType
ACT = mybir.ActivationFunctionType
AX_X = mybir.AxisListType.X

P = 128
B, S, D = 64, 128, 256
C = D // P
L, H, DFF = 3, 8, 1024
DK = D // H
FC = DFF // P
XH = 16
XDK = D // XH
G = 4
GROUPS = B // G
T = G * S
UH = 8
UW = UH * S
BANK = 512
FIRST_KEY_MASK = [1, 1, 0]
FFN_LAYERS = [0, 2]
EPS = 1e-5
MASKED = -1e30
ROOT_FLOOR = 1e-19
SCALE = DK ** -0.5
XSCALE = XDK ** -0.5
PAD_BIAS = 1e10 / XSCALE
SEED = 1

L_UNITS = L * G
X_UNITS = G * XH // UH
UNITS = L_UNITS + X_UNITS


class Ring:

    def __init__(self, names, depth):
        assert len(names) % depth == 0 and len(set(names)) == len(names)
        self.at = {n: i for i, n in enumerate(names)}
        self.depth = depth
        self.turns = len(names) // depth

    def slot(self, name):
        return self.at[name] % self.depth

    def turn(self, name):
        return self.at[name] // self.depth


def unit_layer(u):
    return u // G if u < L_UNITS else None


def unit_seq(u):
    return u % G if u < L_UNITS else (u - L_UNITS) // C


UNIT_SLOT = {0: 0, 1: 1, 2: 2, 3: 3, 4: 4, 5: 5, 6: 6, 7: 7, 8: 12, 9: 13, 10: 14, 11: 15}
for _i in range(X_UNITS):
    UNIT_SLOT[L_UNITS + _i] = 22 + _i
SLOTS = 35
UNIT_AT = {s: u for u, s in UNIT_SLOT.items()}

DENSE_AT = {
    -1: [("k", 0), ("v", 0), ("k", 1), ("v", 1), ("kx",), ("vx",)],
    6: [("ffn", 0, 0)],
    8: [("ffn", 0, 1)],
    11: [("k", 2), ("v", 2)],
    17: [("ffn", 2, 0)],
    19: [("ffn", 2, 1)],
    21: [("q",)],
}
TURN_AT = {s: [] for s in range(-1, SLOTS)}
for _u in range(L_UNITS):
    TURN_AT[UNIT_SLOT[_u] + 4].append((_u // G, 1, _u % G))
for _l, _p, _s in ((0, 0, 7), (0, 1, 9), (2, 0, 18), (2, 1, 20)):
    TURN_AT[_s] += [(_l, 2, 2 * _p), (_l, 2, 2 * _p + 1)]


def general_uses():
    uses = []
    for s in range(-1, SLOTS):
        u = UNIT_AT.get(s - 2)
        if u is not None:
            uses.append(("att", u))
        u = UNIT_AT.get(s - 3)
        if u is not None and (u < L_UNITS or (u - L_UNITS) % C == 1):
            uses.append(("o", u))
        for key in TURN_AT[s]:
            uses.append(("turn",) + key)
        for step in DENSE_AT.get(s, []):
            if step[0] in ("k", "kx", "q"):
                uses += [step + (c,) for c in range(C)]
            elif step[0] in ("v", "vx"):
                uses += [step + (b,) for b in range(G)]
            else:
                uses += [("up",) + step[1:] + (f,) for f in range(FC)]
                uses += [("down",) + step[1:] + (b,) for b in range(2)]
    return uses


def norm_uses():
    uses = []
    for s in range(-1, SLOTS):
        u = UNIT_AT.get(s - 3)
        if u is not None and u < L_UNITS:
            uses.append((u // G, 1, u % G))
        elif u is not None and (u - L_UNITS) % C == 1:
            uses.append((3, 1, unit_seq(u)))
        for step in DENSE_AT.get(s, []):
            if step[0] == "ffn":
                uses += [(step[1], 2, 2 * step[2]), (step[1], 2, 2 * step[2] + 1)]
    return uses


def build(nc, t):
    gen = Ring(general_uses(), 2)
    norms = Ring(norm_uses(), 2)
    NORMS = len(norms.at)

    pad_parts_dram = nc.dram_tensor("pad_parts", (3, B * S), BF16, kind="Internal").ap()
    dam_rows_dram = nc.dram_tensor("dam_rows", (L * H, P, 2 * S), BF16, kind="Internal").ap()

    with ExitStack() as ctx:
        def sb(name, shape, dt=F32):
            return ctx.enter_context(nc.sbuf_tensor(name, shape, dt))

        def sem(name):
            return ctx.enter_context(nc.semaphore(name))

        k_w = [sb(f"k_w{l}", [P, C, D]) for l in range(L)]
        v_w = [sb(f"v_w{l}", [P, C, D]) for l in range(L)]
        o_w = [sb(f"o_w{l}", [P, C, D]) for l in range(L)]
        up_w = {l: sb(f"up_w{l}", [P, C, DFF]) for l in FFN_LAYERS}
        down_w = {l: sb(f"down_w{l}", [P, FC, D]) for l in FFN_LAYERS}
        xq_w, xk_w, xv_w, xo_w = (sb(n, [P, C, D]) for n in ("xq_w", "xk_w", "xv_w", "xo_w"))
        k_bias = sb("k_bias", [P, L, C])
        up_bias = sb("up_bias", [P, 2, FC])
        norm_g = sb("norm_g", [P, 6, D])
        norm_b = sb("norm_b", [P, 6, D])
        ROWS = 9
        row_bias = sb("row_bias", [3, ROWS, D], BF16)
        ident = sb("ident", [P, P])
        ident_bf = sb("ident_bf", [P, P], BF16)
        ones3 = sb("ones3", [3, P], BF16)
        dam_bias = [sb(f"dam_bias{l}", [P, UH, S], BF16) for l in range(L)]
        chain = {m: sb(f"chain{m}", [P, UW], BF16) for m in (0, 1)}
        root_floor = sb("root_floor", [P, 1])
        neg_half = sb("neg_half", [P, 1])
        keep_row = sb("keep_row", [P, 1])
        first_row = sb("first_row", [P, 1])
        ctx_f = sb("ctx_f", [P, C, T])
        x_f = sb("x_f", [P, C, T])
        ctx_t = sb("ctx_t", [P, G, D])
        x_t = sb("x_t", [P, G, D])
        pad_mask = sb("pad_mask", [P, T])
        pad_bias = sb("pad_bias", [3, T], BF16)
        k_f = [sb(f"k_f{i}", [P, C, T]) for i in range(2)]
        xk_f = sb("xk_f", [P, C, T])
        v_t = [sb(f"v_t{i}", [P, G, D]) for i in range(2)]
        xv_t = sb("xv_t", [P, G, XH // 2, 2, 2, XDK])
        k_diag = sb("k_diag", [P, 2, UW])
        xk_diag = sb("xk_diag", [P, 2, UW])
        E = sb("E", [P, UW])
        suffix = sb("suffix", [P, UW + 1])
        X = sb("X", [P, 2, UW])
        probs_f = sb("probs_f", [P, 2, UW])
        att_f = sb("att_f", [P, 2, C, S])
        f_buf = sb("f_buf", [P, C, T])
        h_buf = sb("h_buf", [P, C, T])
        a_tok = sb("a_tok", [P, G, D])
        b_tok = sb("b_tok", [P, G, D])
        y_tok = sb("y_tok", [P, 2, D])
        hidden = sb("hidden", [P, FC, 2 * S])
        out_t = sb("out_t", [P, 2, D])
        res = sb("res", [P, 2, D])
        stats = sb("stats", [P, 2, 6])
        moments = sb("moments", [P, 2, 2])
        rstd = sb("rstd", [P, 2, 1])
        iota_i = sb("iota_i", [P, S], I32)
        pos_f = sb("pos_f", [P, 3, S])
        gam = sb("gam", [P, 4, L * H])
        work = hidden[:, :, :].rearrange("p f n -> p (f n)")
        logits = work[0:L * H, 0:256].rearrange("p (s e) -> p s e", e=2)
        gumbel = work[0:L * H, 256:512].rearrange("p (s e) -> p s e", e=2)
        rows = work[0:ROWS, 512:768]
        rows_parts = work[0:ROWS, 768:1152].bitcast(BF16).rearrange("p (i n) -> p i n", i=3)
        pads = work[0:B, 1152:1280]
        pads_parts = work[0:B, 1280:1472].bitcast(BF16).rearrange("p (i n) -> p i n", i=3)
        dam_rows = work[0:L * H, 1472:1600].bitcast(BF16)
        one_col = sb("one_col", [P, 1])
        eps_col = sb("eps_col", [P, 1])
        m1 = sb("m1", [P, 2, UH])
        nm1 = sb("nm1", [P, 2, UH])
        z1 = sb("z1", [P, 2, UH])
        rz1 = sb("rz1", [P, 2, UH])
        m2 = sb("m2", [P, 2, UH])
        nm2 = sb("nm2", [P, 2, UH])
        z2 = sb("z2", [P, 2, UH])
        rz2 = sb("rz2", [P, 2, UH])

        scores_ps = [ctx.enter_context(nc.psum_tensor(f"scores_ps{i}", [P, UW], F32)) for i in range(2)]
        probs_ps = [ctx.enter_context(nc.psum_tensor(f"probs_ps{i}", [P, BANK], F32)) for i in range(2)]
        gen_ps = [ctx.enter_context(nc.psum_tensor(f"gen_ps{i}", [P, BANK], F32)) for i in range(2)]

        weights_in, setup_in, parts_out, toeplitz_in = (
            sem(n) for n in ("weights_in", "setup_in", "parts_out", "toeplitz_in"))
        pool_step, pool_ready, dve_step, gamma_ready, parts_ready, dve_ready, act_step = (
            sem(n) for n in ("pool_step", "pool_ready", "dve_step", "gamma_ready", "parts_ready", "dve_ready",
                             "act_step"))
        iota_ready, pos_ready, masks_ready = (sem(n) for n in ("iota_ready", "pos_ready", "masks_ready"))
        ctxf_in, xf_in, tok_in, pad_in = (sem(n) for n in ("ctxf_in", "xf_in", "tok_in", "pad_in"))
        gen_full = [sem(f"gen_full{i}") for i in range(2)]
        gen_free = [sem(f"gen_free{i}") for i in range(2)]
        diag_in = [sem(f"diag_in{i}") for i in range(2)]
        xdiag_in = [sem(f"xdiag_in{i}") for i in range(2)]
        scores_done = sem("scores_done")
        scores_free = [sem(f"scores_free{i}") for i in range(2)]
        max1_done, nm1_done, exp1_done, scan_done, recip_done, rz1_done, x_done = (
            sem(n) for n in ("max1_done", "nm1_done", "exp1_done", "scan_done", "recip_done", "rz1_done", "x_done"))
        ln_done, root_done, te_done, select_done, max2_done, nm2_done, exp2_done = (
            sem(n) for n in ("ln_done", "root_done", "te_done", "select_done", "max2_done", "nm2_done", "exp2_done"))
        z2_fixed, rz2_done, norm_done = (sem(n) for n in ("z2_fixed", "rz2_done", "norm_done"))
        pt_full = [sem(f"pt_full{i}") for i in range(2)]
        pt_free = [sem(f"pt_free{i}") for i in range(2)]
        stats_done, moments_done, var_done, rstd_done, scaled_done, tok_done = (
            sem(n) for n in ("stats_done", "moments_done", "var_done", "rstd_done", "scaled_done", "tok_done"))
        passed = sem("passed")
        out_done = [sem(f"out_done{i}") for i in range(2)]
        SETUP_LOADS = 16 * (1 + 2 + ROWS + 1)
        PARTS_OUT = 16 * 7

        def norm_row(key):
            l, which, _ = key
            return 5 if l == 3 else (l if which == 1 else 3 + FFN_LAYERS.index(l))

        def residual(key):
            l, which, b = key
            if which == 2:
                return a_tok[:, b, :]
            return {0: ctx_t, 1: x_t, 2: b_tok, 3: b_tok}[l][:, b, :]

        def norm_out(key):
            l, which, b = key
            if l == 3:
                return out_t[:, b % 2, :]
            if which == 1:
                return {0: a_tok, 1: b_tok, 2: a_tok}[l][:, b, :]
            return y_tok[:, b % 2, :] if l == 0 else b_tok[:, b, :]

        def turn_out(key):
            l, which, b = key
            buf = h_buf if (l == 1 or (l == 2 and which == 2)) else f_buf
            return buf[:, :, b * S:(b + 1) * S]

        def evacuated(eng, g, *names):
            for i in range(2):
                turns = [gen.turn(n) for n in names if gen.slot(n) == i]
                if turns:
                    eng.wait_ge(gen_free[i], g * gen.turns + max(turns) + 1 + SEED)

        def wait_apart(eng, sem_, value):
            eng.wait_ge(sem_, value)
            eng.sem_inc(passed, 1)

        def take(eng, g, name):
            i = gen.slot(name)
            eng.wait_ge(gen_full[i], g * gen.turns + gen.turn(name) + 1)
            return gen_ps[i], gen_free[i]

        def unit_heads(ap):
            return ap.rearrange("p (h k) -> p h k", k=S)

        def has_out(u):
            return u is not None and (u < L_UNITS or (u - L_UNITS) % C == C - 1)

        def out_key(u):
            return (u // G if u < L_UNITS else 3, 1, unit_seq(u))

        block = ctx.enter_context(nc.Block())

        @block.sync
        def _(sp):
            sp.dma_start(gam[:, 0, :], bass.AP(t["gammas"].tensor, 0, [[0, P], [1, L * H]])).then_inc(setup_in, 16)
            sp.dma_start(logits[:, :, :], t["alphas"].rearrange("l h s e -> (l h) s e")).then_inc(setup_in, 16)
            sp.dma_start(gumbel[:, :, :], t["gumbel"].rearrange("l h s e -> (l h) s e")).then_inc(setup_in, 16)
            for i, src in enumerate([t["vb"][0], t["vb"][1], t["vb"][2], t["ob"][0], t["ob"][1], t["ob"][2],
                                     t["b2"][0], t["b2"][2], t["bo"]]):
                sp.dma_start(rows[i:i + 1, :], src.unsqueeze(0)).then_inc(setup_in, 16)
            sp.dma_start(pads[:, :], t["pad"]).then_inc(setup_in, 16)
            n_w = 0
            for l in range(L):
                for dst, name in ((k_w, "kWT"), (v_w, "vWT"), (o_w, "oWT")):
                    sp.dma_start(dst[l][:, :, :], t[name][l].rearrange("(c p) n -> p c n", p=P)).then_inc(weights_in, 16)
                n_w += 3
            sp.dma_start(k_bias[:, :, :], t["kb"]).then_inc(weights_in, 16)
            sp.dma_start(up_bias[:, :, :], t["b1"]).then_inc(weights_in, 16)
            n_w += 2
            for i, l in enumerate(FFN_LAYERS):
                sp.dma_start(up_w[l][:, :, :], t["w1T"][l].rearrange("(c p) n -> p c n", p=P)).then_inc(weights_in, 16)
                sp.dma_start(down_w[l][:, :, :], t["w2T"][l].rearrange("(c p) n -> p c n", p=P)).then_inc(weights_in, 16)
                n_w += 2
            for dst, name in ((xq_w, "wq"), (xk_w, "wk"), (xv_w, "wv"), (xo_w, "wo")):
                sp.dma_start(dst[:, :, :], t[name].rearrange("(c p) n -> p c n", p=P)).then_inc(weights_in, 16)
                n_w += 1
            for dst, srcs in ((norm_g, [t["ln1_g"][0], t["ln1_g"][1], t["ln1_g"][2], t["ln2_g"][0], t["ln2_g"][2],
                                        t["ln_gamma"]]),
                              (norm_b, [t["ln1_b"][0], t["ln1_b"][1], t["ln1_b"][2], t["ln2_b"][0], t["ln2_b"][2],
                                        t["ln_beta"]])):
                for i, src in enumerate(srcs):
                    sp.dma_start(dst[:, i, :], bass.AP(src.tensor, src.offset, [[0, P], [1, D]])).then_inc(weights_in, 16)
                    n_w += 1
            assert n_w == N_WEIGHTS

            sp.wait_ge(parts_ready, 3)
            for i in range(3):
                sp.dma_start(row_bias[i:i + 1, :, :], rows_parts[:, i, :]).then_inc(parts_out, 16)
                sp.dma_start(pad_parts_dram[i].rearrange("(b s) -> b s", b=B), pads_parts[:, i, :]).then_inc(parts_out, 16)
            sp.dma_start(dam_rows_dram, dam_rows[:, :].unsqueeze(1).to_broadcast([L * H, P, 2 * S])).then_inc(parts_out, 16)
            sp.wait_ge(parts_out, PARTS_OUT)
            for l in range(L):
                src = bass.AP(dam_rows_dram.tensor, l * H * P * 2 * S + S, [[2 * S - 1, P], [P * 2 * S, H], [1, S]])
                sp.dma_start(dam_bias[l][:, :, :], src).then_inc(toeplitz_in, 16)
            sp.wait_ge(masks_ready, 2)

            def diag_blocks(u):
                b, slot = unit_seq(u), u % 2
                if u < L_UNITS:
                    for c in range(C):
                        for j in range(P // DK):
                            rows_j = slice(j * DK, (j + 1) * DK)
                            col = c * BANK + j * S
                            sp.dma_start(k_diag[rows_j, slot, col:col + S],
                                         k_f[unit_layer(u) % 2][rows_j, c, b * S:(b + 1) * S]).then_inc(diag_in[slot], 16)
                else:
                    c = (u - L_UNITS) % C
                    for j in range(UH):
                        rows_j = slice(j * XDK, (j + 1) * XDK)
                        sp.dma_start(xk_diag[rows_j, slot, j * S:(j + 1) * S],
                                     xk_f[rows_j, c, b * S:(b + 1) * S]).then_inc(xdiag_in[slot], 16)

            with sp.Fori(0, GROUPS) as g:
                tok = bass.ds(g * T, T)
                wait_apart(sp, scores_done, g * UNITS + SEED)
                sp.dma_start(ctx_f[:, :, :], t["ctxT"][:, tok].rearrange("(c p) n -> p c n", p=P)).then_inc(ctxf_in, 16)
                sp.dma_start(x_f[:, :, :], t["xT"][:, tok].rearrange("(c p) n -> p c n", p=P)).then_inc(xf_in, 16)
                sp.dma_start(pad_mask[:, :], bass.AP(t["pad"].tensor, g * T, [[0, P], [1, T]])).then_inc(pad_in, 16)
                sp.dma_start(pad_bias[:, :], pad_parts_dram[:, tok]).then_inc(pad_in, 16)
                sp.dma_start(ctx_t[:, :, :], t["ctx"][tok, :].rearrange("(b s) d -> s b d", s=S)).then_inc(tok_in, 16)
                sp.dma_start(x_t[:, :, :], t["x"][tok, :].rearrange("(b s) d -> s b d", s=S)).then_inc(tok_in, 16)
                for s in range(-1, SLOTS):
                    u = UNIT_AT.get(s + 1)
                    if u is not None:
                        for c in range(C):
                            evacuated(sp, g, ("kx", c) if u >= L_UNITS else ("k", unit_layer(u), c))
                            sp.sem_inc(passed, 1)
                        wait_apart(sp, scores_done, g * UNITS + max(u - 1, 0) + SEED)
                        diag_blocks(u)
                    u = UNIT_AT.get(s - 4)
                    if has_out(u) and u >= L_UNITS:
                        b = unit_seq(u)
                        wait_apart(sp, tok_done, g * NORMS + norms.at[(3, 1, b)] + 1)
                        sp.dma_start(t["out"][bass.ds(g * T + b * S, S), :], out_t[:, b % 2, :]
                                     ).then_inc(out_done[b % 2], 16)
            for i in range(2):
                sp.wait_ge(out_done[i], 16 * GROUPS * G // 2 + SEED)

        @block.tensor
        def _(pe):
            pe.wait_ge(weights_in, 16 * N_WEIGHTS)
            pe.wait_ge(parts_out, PARTS_OUT)
            pe.wait_ge(dve_ready, 1)
            pe.wait_ge(masks_ready, 2)
            pe.wait_ge(pool_ready, 1)

            def general(g, name, *needs):
                i = gen.slot(name)
                pe.wait_ge(gen_free[i], g * gen.turns + gen.turn(name) + SEED)
                evacuated(pe, g, *[n for n in needs if gen.slot(n) != i])
                return gen_ps[i], gen_full[i]

            def add_row(out, row):
                return nc.tensor.matmul(out, ones3[:, :], row_bias[:, row, :], start=False, stop=True)

            def feature_major(g, step, w, src, *needs):
                for c in range(C):
                    ps, full = general(g, step + (c,), *(needs if c == 0 else ()))
                    for k in range(C):
                        mm = nc.tensor.matmul(ps[:, :], w[:, k, c * P:(c + 1) * P], src[:, k, :], start=(k == 0),
                                              stop=(k == C - 1))
                    mm.then_inc(full, 1)

            def token_major(g, step, w, src, row, *needs):
                for b in range(G):
                    ps, full = general(g, step + (b,), *(needs if b == 0 else ()))
                    for k in range(C):
                        mm = nc.tensor.matmul(ps[:, 0:D], src[:, k, b * S:(b + 1) * S], w[:, k, :], start=(k == 0),
                                              stop=(k == C - 1 and row is None))
                    if row is not None:
                        mm = add_row(ps[:, 0:D], row)
                    mm.then_inc(full, 1)

            def feed_forward(g, l, pair):
                for f in range(FC):
                    needs = [("turn", l, 1, b) for b in (2 * pair, 2 * pair + 1)] if f == 0 else []
                    ps, full = general(g, ("up", l, pair, f), *needs)
                    for k in range(C):
                        mm = nc.tensor.matmul(ps[:, 0:2 * S], up_w[l][:, k, f * P:(f + 1) * P],
                                              f_buf[:, k, pair * 2 * S:(pair + 1) * 2 * S], start=(k == 0),
                                              stop=(k == C - 1))
                    mm.then_inc(full, 1)
                for b in range(2):
                    ps, full = general(g, ("down", l, pair, b))
                    for f in range(FC):
                        if b == 0 and f == FC - 1:
                            evacuated(pe, g, ("up", l, pair, FC - 2), ("up", l, pair, FC - 1))
                        nc.tensor.matmul(ps[:, 0:D], hidden[:, f, b * S:(b + 1) * S], down_w[l][:, f, :],
                                         start=(f == 0), stop=False)
                    add_row(ps[:, 0:D], 6 + FFN_LAYERS.index(l)).then_inc(full, 1)

            def dense(g, step):
                kind = step[0]
                if kind == "k":
                    l = step[1]
                    if l == 0:
                        pe.wait_ge(ctxf_in, 16 * (g + 1))
                    elif l == 1:
                        pe.wait_ge(xf_in, 16 * (g + 1))
                    needs = [("turn", 1, 1, b) for b in range(G)] if l == 2 else []
                    feature_major(g, step, k_w[l], (ctx_f, x_f, h_buf)[l], *needs)
                elif kind == "v":
                    l = step[1]
                    needs = [("turn", 0, 2, b) for b in range(G)] if l == 2 else []
                    token_major(g, step, v_w[l], (ctx_f, x_f, f_buf)[l], l, *needs)
                elif kind == "kx":
                    feature_major(g, step, xk_w, ctx_f)
                elif kind == "vx":
                    token_major(g, step, xv_w, ctx_f, None)
                elif kind == "q":
                    feature_major(g, step, xq_w, h_buf, *[("turn", 2, 2, b) for b in range(G)])
                else:
                    feed_forward(g, step[1], step[2])

            def scores(g, u):
                p, b = u % 2, unit_seq(u)
                out = scores_ps[p]
                pe.wait_ge(scores_free[p], g * (UNITS // 2) + u // 2 + SEED)
                if u < L_UNITS:
                    l = unit_layer(u)
                    pe.wait_ge(diag_in[p], (g * (L_UNITS // 2) + u // 2 + 1) * 16 * UH)
                    for c in range(C):
                        half = slice(c * BANK, (c + 1) * BANK)
                        nc.tensor.matmul(out[:, half], k_f[l % 2][:, c, b * S:(b + 1) * S], k_diag[:, p, half],
                                         start=True, stop=False)
                        mm = nc.tensor.matmul(out[:, half], ident_bf[:, :],
                                              dam_bias[l][:, c * 4:(c + 1) * 4, :].rearrange("p h k -> p (h k)"),
                                              start=False, stop=True)
                else:
                    i = u - L_UNITS
                    pe.wait_ge(xdiag_in[p], (g * (X_UNITS // 2) + i // 2 + 1) * 16 * UH)
                    pe.wait_ge(pad_in, 32 * (g + 1))
                    evacuated(pe, g, ("q", i % C))
                    for half in range(2):
                        cols = slice(half * BANK, (half + 1) * BANK)
                        nc.tensor.matmul(out[:, cols], f_buf[:, i % C, b * S:(b + 1) * S], xk_diag[:, p, cols],
                                         start=True, stop=False)
                        bias = pad_bias[:, b * S:(b + 1) * S].unsqueeze(1).to_broadcast([3, BANK // S, S])
                        mm = nc.tensor.matmul(out[:, cols], ones3[:, :], bias, start=False, stop=True)
                mm.then_inc(scores_done, 1)

            def probs_turn(g, u):
                p = u % 2
                pe.wait_ge(norm_done, g * UNITS + u + 1)
                for half in range(2):
                    pe.wait_ge(pt_free[half], g * UNITS + u + SEED)
                    for j in range(4):
                        h = half * 4 + j
                        mm = nc.tensor.transpose(probs_ps[half][:, j * S:(j + 1) * S], X[:, p, h * S:(h + 1) * S],
                                                 ident[:, :])
                    mm.then_inc(pt_full[half], 1)

            def attend(g, u):
                p, b = u % 2, unit_seq(u)
                ps, full = general(g, ("att", u), ("v", unit_layer(u), b) if u < L_UNITS else ("vx", b))
                for half in range(2):
                    pe.wait_ge(pt_free[half], g * UNITS + u + 1 + SEED)
                    for j in range(4):
                        h = half * 4 + j
                        probs = probs_f[:, p, h * S:(h + 1) * S]
                        if u < L_UNITS:
                            mm = nc.tensor.matmul(ps[j * DK:(j + 1) * DK, half * S:(half + 1) * S],
                                                  v_t[unit_layer(u) % 2][:, b, h * DK:(h + 1) * DK], probs,
                                                  start=True, stop=True)
                        else:
                            pair, e = h // 2, h % 2
                            v = xv_t[:, b, (u - L_UNITS) % C * 4 + pair, e, :, :].rearrange("p e d -> p (e d)")
                            mm = nc.tensor.matmul(ps[pair * 32:(pair + 1) * 32, 0:S], v, probs,
                                                  start=(e == 0), stop=(e == 1))
                mm.then_inc(full, 1)

            def out_proj(g, u):
                b = unit_seq(u)
                ps, full = general(g, ("o", u), ("att", u), *([("att", u - 1)] if u >= L_UNITS else []))
                w, row = (o_w[unit_layer(u)], 3 + unit_layer(u)) if u < L_UNITS else (xo_w, 8)
                for c in range(C):
                    nc.tensor.matmul(ps[:, 0:D], att_f[:, b % 2, c, :], w[:, c, :], start=(c == 0), stop=False)
                add_row(ps[:, 0:D], row).then_inc(full, 1)

            def turn(g, key):
                ps, full = general(g, ("turn",) + key)
                pe.wait_ge(tok_done, g * NORMS + norms.at[key] + 1)
                for c in range(C):
                    mm = nc.tensor.transpose(ps[:, c * S:(c + 1) * S], norm_out(key)[:, c * P:(c + 1) * P], ident[:, :])
                mm.then_inc(full, 1)

            with pe.Fori(0, GROUPS) as g:
                for s in range(-1, SLOTS):
                    if s in UNIT_AT:
                        scores(g, UNIT_AT[s])
                    if s - 2 in UNIT_AT:
                        probs_turn(g, UNIT_AT[s - 2])
                        attend(g, UNIT_AT[s - 2])
                    if has_out(UNIT_AT.get(s - 3)):
                        out_proj(g, UNIT_AT[s - 3])
                    for key in TURN_AT[s]:
                        turn(g, key)
                    for step in DENSE_AT.get(s, []):
                        dense(g, step)

        @block.scalar
        def _(act):
            nc.scalar.preload_act_table_set("natural_log_exp_and_others")
            act.wait_ge(pool_ready, 1)
            act.wait_ge(gamma_ready, 1)
            nc.scalar.activation(gam[:, 1, :], gam[:, 1, :], ACT.Exp, scale=-1.0).then_inc(act_step, 1)
            act.wait_ge(act_step, 1)
            nc.scalar.activation(gam[:, 1, :], gam[:, 1, :], ACT.Ln, bias=one_col[:, :]).then_inc(act_step, 1)
            nc.scalar.activation(gumbel[:, :, :], gumbel[:, :, :], ACT.Ln, bias=eps_col[0:L * H, :]).then_inc(act_step, 1)
            act.wait_ge(weights_in, 16 * N_WEIGHTS)
            act.wait_ge(dve_ready, 1)

            def keys(g, l):
                for c in range(C):
                    ps, free = take(act, g, ("k", l, c))
                    nc.scalar.activation(k_f[l % 2][:, c, :], ps[:, :], ACT.Identity, bias=k_bias[:, l, c:c + 1]
                                         ).then_inc(free, 1)

            def exps(src, minus_max, dst, sums, scale, done):
                for h in range(UH):
                    cols = slice(h * S, (h + 1) * S)
                    a = nc.scalar.activation(dst[:, cols], src[:, cols], ACT.Exp, bias=minus_max[:, h:h + 1], scale=scale,
                                             accum_out=sums[:, h:h + 1])
                a.then_inc(done, 1)

            def exp1(g, u):
                p = u % 2
                act.wait_ge(nm1_done, g * UNITS + u + 1)
                if u < L_UNITS:
                    act.wait_ge(scan_done, g * L_UNITS + u + SEED)
                    exps(scores_ps[p], nm1[:, p, :], E[:, :], z1[:, p, :], SCALE, exp1_done)
                else:
                    act.wait_ge(pt_full[1], g * UNITS + u - 1 + SEED)
                    exps(scores_ps[p], nm1[:, p, :], X[:, p, :], z2[:, p, :], XSCALE, scores_free[p])

            def effect(g, u):
                n = g * L_UNITS + u
                x = X[:, u % 2, :]
                act.wait_ge(x_done, n + 1 + SEED)
                nc.scalar.activation(x, x, ACT.Ln, bias=root_floor[:, :]).then_inc(ln_done, 1)
                act.wait_ge(ln_done, n + 1)
                nc.scalar.activation(x, x, ACT.Exp, scale=0.5).then_inc(root_done, 1)
                act.wait_ge(root_done, n + 1)
                nc.scalar.activation(x, x, ACT.Exp, scale=-1.0).then_inc(te_done, 1)

            def exp2(g, u):
                p = u % 2
                act.wait_ge(nm2_done, g * L_UNITS + u + 1)
                exps(X[:, p, :], nm2[:, p, :], X[:, p, :], z2[:, p, :], SCALE, exp2_done)

            def probs_copy(g, u):
                for half in range(2):
                    act.wait_ge(pt_full[half], g * UNITS + u + 1 + SEED)
                    nc.scalar.copy(probs_f[:, u % 2, half * BANK:(half + 1) * BANK], probs_ps[half][:, :]
                                   ).then_inc(pt_free[half], 1)

            def att_copy(g, u):
                ps, free = take(act, g, ("att", u))
                b = unit_seq(u)
                if u < L_UNITS:
                    dst, src = att_f[:, b % 2, :, :].rearrange("p c s -> p (c s)"), ps[:, 0:C * S]
                else:
                    dst, src = att_f[:, b % 2, (u - L_UNITS) % C, :], ps[:, 0:S]
                nc.scalar.copy(dst, src).then_inc(free, 1)

            def hidden_layer(g, l, pair):
                i = FFN_LAYERS.index(l)
                for f in range(FC):
                    ps, free = take(act, g, ("up", l, pair, f))
                    nc.scalar.activation(hidden[:, f, :], ps[:, 0:2 * S], ACT.Relu, bias=up_bias[:, i, f:f + 1]
                                         ).then_inc(free, 1)

            with act.Fori(0, GROUPS) as g:
                for s in range(-1, SLOTS):
                    last = UNIT_AT.get(s - 1)
                    if last is not None and last < L_UNITS:
                        effect(g, last)
                    if s in UNIT_AT:
                        exp1(g, UNIT_AT[s])
                    if s - 2 in UNIT_AT:
                        probs_copy(g, UNIT_AT[s - 2])
                    if last is not None and last < L_UNITS:
                        exp2(g, last)
                    if s - 2 in UNIT_AT:
                        att_copy(g, UNIT_AT[s - 2])
                    for step in DENSE_AT.get(s, []):
                        if step[0] == "k":
                            keys(g, step[1])
                        if step[0] == "ffn":
                            hidden_layer(g, step[1], step[2])

        @block.vector
        def _(dve):
            steps = [0]

            def link(ins):
                steps[0] += 1
                ins.then_inc(dve_step, 1)
                dve.wait_ge(dve_step, steps[0])

            dve.wait_ge(setup_in, SETUP_LOADS)
            link(nc.vector.tensor_scalar(gam[:, 3, :], gam[:, 0, :], -1.0, None, ALU.mult))
            link(nc.vector.tensor_scalar(gam[:, 2, :], gam[:, 0, :], 0.0, None, ALU.max))
            nc.vector.tensor_tensor(gam[:, 1, :], gam[:, 0, :], gam[:, 3, :], ALU.max).then_inc(gamma_ready, 1)
            link(nc.vector.tensor_scalar(pads[:, :], pads[:, :], -1.0, PAD_BIAS, ALU.add, ALU.mult))
            for whole, parts in ((pads, pads_parts), (rows, rows_parts)):
                for i in range(3):
                    ins = nc.vector.tensor_copy(parts[:, i, :], whole[:, :])
                    if i < 2:
                        link(ins)
                        link(nc.vector.tensor_tensor(whole[:, :], whole[:, :], parts[:, i, :], ALU.subtract))
                    else:
                        ins.then_inc(parts_ready, 1)
            dve.wait_ge(act_step, 3)
            link(nc.vector.tensor_tensor(logits[:, :, :], logits[:, :, :], gumbel[:, :, :], ALU.subtract))
            link(nc.vector.tensor_tensor(gumbel[:, :, 0], logits[:, :, 0], logits[:, :, 1], ALU.is_ge))
            link(nc.vector.memset(dam_rows[:, 0:S], 0.0))
            link(nc.vector.tensor_scalar(dam_rows[:, S:2 * S], gumbel[:, :, 0], MASKED, None, ALU.mult))
            nc.vector.memset(dam_rows[0:2 * H, S:S + 1], 0.0).then_inc(parts_ready, 1)
            link(nc.vector.tensor_tensor(gam[:, 1, :], gam[:, 1, :], gam[:, 2, :], ALU.add))
            link(nc.vector.tensor_tensor(gam[:, 1, :], gam[:, 1, :], gam[:, 1, :], ALU.mult))
            dve.wait_ge(iota_ready, 1)
            nc.vector.tensor_copy(pos_f[:, 2, :], iota_i[:, :]).then_inc(pos_ready, 1)
            dve.wait_ge(masks_ready, 1)
            for m in (0, 1):
                for h in range(UH):
                    link(nc.vector.tensor_scalar(chain[m][:, h * S:(h + 1) * S], pos_f[:, m, :], 0.0, None, ALU.is_gt))
            link(nc.vector.tensor_copy(ident_bf[:, :], ident[:, :]))
            dve.wait_ge(toeplitz_in, 16 * L)
            nc.vector.memset(dam_bias[2][0:1, :, 0:1], 0.0).then_inc(dve_ready, 1)
            dve.wait_ge(weights_in, 16 * N_WEIGHTS)
            dve.wait_ge(pool_ready, 1)

            def max1(g, u):
                p = u % 2
                n = g * UNITS + u + 1
                dve.wait_ge(scores_done, n + SEED)
                nc.vector.tensor_reduce(m1[:, p, :], unit_heads(scores_ps[p][:, :]), AX_X, ALU.max).then_inc(max1_done, 1)
                dve.wait_ge(max1_done, n)
                nc.vector.tensor_scalar(nm1[:, p, :], m1[:, p, :], -(SCALE if u < L_UNITS else XSCALE), None, ALU.mult
                                        ).then_inc(nm1_done, 1)

            def distance(g, u):
                p, n, l = u % 2, g * L_UNITS + u, unit_layer(u)
                dve.wait_ge(exp1_done, n + 1)
                nc.vector.reciprocal(rz1[:, p, :], z1[:, p, :]).then_inc(recip_done, 1)
                dve.wait_ge(x_done, n + SEED)
                nc.vector.tensor_tensor_scan(suffix[:, UW - 1::-1], chain[FIRST_KEY_MASK[l]][:, ::-1], E[:, ::-1], 0.0,
                                             ALU.mult, ALU.add).then_inc(scan_done, 1)
                dve.wait_ge(recip_done, n + 1)
                nc.vector.tensor_tensor(rz1[:, p, :], rz1[:, p, :], gam[:, 1, l * H:(l + 1) * H], ALU.mult
                                        ).then_inc(rz1_done, 1)
                dve.wait_ge(rz1_done, n + 1)
                dve.wait_ge(scan_done, n + 1 + SEED)
                dve.wait_ge(pt_full[1], g * UNITS + max(u - 1, 0) + SEED)
                for h in range(UH):
                    ins = nc.vector.scalar_tensor_tensor(out=X[:, p, h * S:(h + 1) * S],
                                                         in0=suffix[:, h * S + 1:(h + 1) * S + 1],
                                                         scalar=rz1[:, p, h:h + 1], in1=pos_f[:, FIRST_KEY_MASK[l], :], op0=ALU.mult,
                                                         op1=ALU.mult)
                ins.then_inc(x_done, 1)

            def scores2(g, u):
                p = u % 2
                dve.wait_ge(te_done, g * L_UNITS + u + 1)
                nc.vector.scalar_tensor_tensor(out=X[:, p, :], in0=X[:, p, :], scalar=1e-5, in1=scores_ps[p][:, :],
                                               op0=ALU.max, op1=ALU.mult).then_inc(scores_free[p], 1)

            def max2(g, u):
                p, n = u % 2, g * L_UNITS + u + 1
                dve.wait_ge(select_done, n)
                nc.vector.tensor_reduce(m2[:, p, :], unit_heads(X[:, p, :]), AX_X, ALU.max).then_inc(max2_done, 1)
                dve.wait_ge(max2_done, n)
                keep = keep_row[:, 0:1] if unit_layer(u) == 2 else 1.0
                nc.vector.tensor_scalar(nm2[:, p, :], m2[:, p, :], -SCALE, keep, ALU.mult, ALU.mult
                                        ).then_inc(nm2_done, 1)

            def normalise(g, u):
                p = u % 2
                if u < L_UNITS:
                    dve.wait_ge(exp2_done, g * L_UNITS + u + 1)
                else:
                    dve.wait_ge(scores_free[p], g * (UNITS // 2) + u // 2 + 1 + SEED)
                if unit_layer(u) == 2:
                    nc.vector.tensor_scalar(z2[:, p, :], z2[:, p, :], first_row[:, 0:1], None, ALU.add
                                            ).then_inc(z2_fixed, 1)
                    dve.wait_ge(z2_fixed, g * G + unit_seq(u) + 1)
                nc.vector.reciprocal(rz2[:, p, :], z2[:, p, :]).then_inc(rz2_done, 1)
                dve.wait_ge(rz2_done, g * UNITS + u + 1)
                nc.vector.tensor_tensor(unit_heads(X[:, p, :]), unit_heads(X[:, p, :]),
                                        rz2[:, p, :].unsqueeze(2).to_broadcast([P, UH, S]), ALU.mult
                                        ).then_inc(norm_done, 1)

            def layer_norm(g, name, key):
                i, n = norms.slot(key), g * NORMS + norms.at[key] + 1
                ps, free = take(dve, g, name)
                nc.vector.tensor_tensor(res[:, i, :], ps[:, 0:D], residual(key), ALU.add).then_inc(free, 1)
                evacuated(dve, g, name)
                nc.vector.bn_stats(stats[:, i, :], res[:, i, :]).then_inc(stats_done, 1)
                wait_apart(dve, stats_done, n)
                nc.vector.bn_aggr(moments[:, i, :], stats[:, i, :]).then_inc(moments_done, 1)
                dve.wait_ge(moments_done, n)
                row = norm_row(key)
                nc.vector.scalar_tensor_tensor(out=res[:, i, :], in0=res[:, i, :], scalar=moments[:, i, 0:1],
                                               in1=norm_g[:, row, :], op0=ALU.subtract, op1=ALU.mult
                                               ).then_inc(scaled_done, 1)
                dve.wait_ge(scaled_done, n)
                dve.wait_ge(rstd_done, n)
                if key[0] == 3:
                    dve.wait_ge(out_done[key[2] % 2], 16 * (g * (G // 2) + key[2] // 2) + SEED)
                nc.vector.scalar_tensor_tensor(out=norm_out(key), in0=res[:, i, :], scalar=rstd[:, i, 0:1],
                                               in1=norm_b[:, row, :], op0=ALU.mult, op1=ALU.add).then_inc(tok_done, 1)

            def turned(g, key):
                ps, free = take(dve, g, ("turn",) + key)
                nc.vector.tensor_copy(turn_out(key), ps[:, 0:C * S].rearrange("p (c s) -> p c s", c=C)).then_inc(free, 1)

            def dense(g, step):
                kind = step[0]
                if kind == "v":
                    for b in range(G):
                        ps, free = take(dve, g, step + (b,))
                        nc.vector.tensor_copy(v_t[step[1] % 2][:, b, :], ps[:, 0:D]).then_inc(free, 1)
                elif kind == "kx":
                    dve.wait_ge(pad_in, 32 * (g + 1))
                    for c in range(C):
                        ps, free = take(dve, g, step + (c,))
                        nc.vector.tensor_tensor(xk_f[:, c, :], ps[:, :], pad_mask[:, :], ALU.mult).then_inc(free, 1)
                elif kind == "vx":
                    for b in range(G):
                        ps, free = take(dve, g, step + (b,))
                        heads = ps[:, 0:D].rearrange("p (q e d) -> p q e d", e=2, d=XDK)
                        for e in range(2):
                            ins = nc.vector.tensor_copy(xv_t[:, b, :, e, e, :], heads[:, :, e, :])
                        ins.then_inc(free, 1)
                elif kind == "q":
                    for c in range(C):
                        ps, free = take(dve, g, step + (c,))
                        nc.vector.tensor_copy(f_buf[:, c, :], ps[:, :]).then_inc(free, 1)
                elif kind == "ffn":
                    _, l, pair = step
                    for b in range(2):
                        layer_norm(g, ("down", l, pair, b), (l, 2, 2 * pair + b))

            with dve.Fori(0, GROUPS) as g:
                dve.wait_ge(tok_in, 32 * (g + 1))
                for s in range(-1, SLOTS):
                    u, last = UNIT_AT.get(s), UNIT_AT.get(s - 1)
                    if u is not None:
                        max1(g, u)
                    if last is not None and last < L_UNITS:
                        scores2(g, last)
                        max2(g, last)
                    if u is not None and u < L_UNITS:
                        distance(g, u)
                    if last is not None:
                        normalise(g, last)
                    if has_out(UNIT_AT.get(s - 3)):
                        layer_norm(g, ("o", UNIT_AT[s - 3]), out_key(UNIT_AT[s - 3]))
                    for key in TURN_AT[s]:
                        turned(g, key)
                    for step in DENSE_AT.get(s, []):
                        dense(g, step)

        @block.gpsimd
        def _(pool):
            n_pool = [0]

            def link(ins):
                n_pool[0] += 1
                ins.then_inc(pool_step, 1)
                pool.wait_ge(pool_step, n_pool[0])

            for seeded in (*gen_free, *scores_free, *pt_free, *pt_full, *out_done, scores_done, scan_done, x_done):
                pool.sem_inc(seeded, SEED)
            nc.gpsimd.iota(iota_i[:, :], [[-1, S]], base=0, channel_multiplier=1).then_inc(iota_ready, 1)
            for tile, value in ((root_floor, ROOT_FLOOR), (neg_half, -0.5), (one_col, 1.0), (eps_col, 1e-5),
                                (keep_row, 1.0), (first_row, 0.0), (ident, 0.0), (ones3, 1.0)):
                link(nc.gpsimd.memset(tile[:, :], value))
            link(nc.gpsimd.memset(keep_row[0:1, :], 0.0))
            link(nc.gpsimd.memset(first_row[0:1, :], 1.0))
            link(nc.gpsimd.memset(suffix[:, UW:UW + 1], 0.0))
            link(nc.gpsimd.affine_select(out=ident[:, :], in_=ident[:, :], compare_op=ALU.not_equal, fill=1.0, base=0,
                                         pattern=[[-1, P]], channel_multiplier=1))
            nc.gpsimd.memset(xv_t[:, :, :, :, :, :], 0.0).then_inc(pool_ready, 1)
            pool.wait_ge(pos_ready, 1)
            for m in (0, 1):
                ins = nc.gpsimd.affine_select(out=pos_f[:, m, :], in_=pos_f[:, 2, :], compare_op=ALU.is_gt, fill=0.0,
                                              base=m - 1, pattern=[[-1, S]], channel_multiplier=1)
                if m == 0:
                    link(ins)
            ins.then_inc(masks_ready, 1)
            link(nc.gpsimd.memset(k_diag[:, :, :], 0.0))
            nc.gpsimd.memset(xk_diag[:, :, :], 0.0).then_inc(masks_ready, 1)

            def select(g, u):
                p, m = u % 2, FIRST_KEY_MASK[unit_layer(u)]
                wait_apart(pool, scores_free[p], g * (UNITS // 2) + u // 2 + 1 + SEED)
                x = unit_heads(X[:, p, :])
                nc.gpsimd.affine_select(out=x, in_=x, compare_op=ALU.is_gt, fill=MASKED, base=m,
                                        pattern=[[0, UH], [-1, S]], channel_multiplier=1).then_inc(select_done, 1)

            def deviation(g, key):
                i, n = norms.slot(key), g * NORMS + norms.at[key] + 1
                pool.wait_ge(moments_done, n)
                nc.gpsimd.tensor_tensor(rstd[:, i, :], moments[:, i, 1:2], eps_col[:, :], ALU.add).then_inc(var_done, 1)
                pool.wait_ge(var_done, n)
                nc.gpsimd.tensor_tensor(rstd[:, i, :], rstd[:, i, :], neg_half[:, :], ALU.pow).then_inc(rstd_done, 1)

            with pool.Fori(0, GROUPS) as g:
                for s in range(-1, SLOTS):
                    last = UNIT_AT.get(s - 1)
                    if last is not None and last < L_UNITS:
                        select(g, last)
                    if has_out(UNIT_AT.get(s - 3)):
                        deviation(g, out_key(UNIT_AT[s - 3]))
                    for step in DENSE_AT.get(s, []):
                        if step[0] == "ffn":
                            for b in range(2):
                                deviation(g, (step[1], 2, 2 * step[2] + b))


N_WEIGHTS = 3 * L + 2 + 2 * len(FFN_LAYERS) + 4 + 12


def kernel(x, ctx_1024, mask_BxS2_ff1, L0_xattn_kW, L0_xattn_kb, L0_xattn_vW, L0_xattn_vb, L0_xattn_oW, L0_xattn_ob,
           L0_xattn_gammas, L0_xattn_alphas, L0_xattn_ln1_g, L0_xattn_ln1_b, L0_xattn_w1, L0_xattn_b1, L0_xattn_w2,
           L0_xattn_b2, L0_xattn_ln2_g, L0_xattn_ln2_b, L0_xattn_gumbel_E, L1_xattn_wq, L1_xattn_wk, L1_xattn_wv,
           L1_xattn_wo, L1_xattn_bo, L1_xattn_ln_gamma, L1_xattn_ln_beta):
    import numpy as np
    import concourse.bacc as bacc
    from concourse.bass_utils import run_bass_kernel_spmd

    arr = np.ascontiguousarray
    x, c = np.asarray(x), np.asarray(ctx_1024)
    data = {
        "x": arr(x.reshape(B * S, D)), "ctx": arr(c.reshape(B * S, D)),
        "xT": arr(x.reshape(B * S, D).T), "ctxT": arr(c.reshape(B * S, D).T),
        "pad": arr(np.asarray(mask_BxS2_ff1)),
        "kWT": arr(np.asarray(L0_xattn_kW).transpose(0, 2, 1)), "vWT": arr(np.asarray(L0_xattn_vW).transpose(0, 2, 1)),
        "oWT": arr(np.asarray(L0_xattn_oW).transpose(0, 2, 1)), "w1T": arr(np.asarray(L0_xattn_w1).transpose(0, 2, 1)),
        "w2T": arr(np.asarray(L0_xattn_w2).transpose(0, 2, 1)),
        "kb": arr(np.asarray(L0_xattn_kb).reshape(L, C, P).transpose(2, 0, 1)),
        "b1": arr(np.asarray(L0_xattn_b1)[FFN_LAYERS].reshape(2, FC, P).transpose(2, 0, 1)),
        "vb": L0_xattn_vb, "ob": L0_xattn_ob, "b2": L0_xattn_b2,
        "gammas": L0_xattn_gammas, "alphas": L0_xattn_alphas, "gumbel": L0_xattn_gumbel_E,
        "ln1_g": L0_xattn_ln1_g, "ln1_b": L0_xattn_ln1_b, "ln2_g": L0_xattn_ln2_g, "ln2_b": L0_xattn_ln2_b,
        "wq": L1_xattn_wq, "wk": L1_xattn_wk, "wv": L1_xattn_wv, "wo": L1_xattn_wo, "bo": L1_xattn_bo,
        "ln_gamma": L1_xattn_ln_gamma, "ln_beta": L1_xattn_ln_beta,
    }
    data = {f"in_{n}": arr(a) for n, a in data.items()}
    nc = bacc.Bacc("TRN2", target_bir_lowering=False, num_devices=1)
    t = {n[3:]: nc.dram_tensor(n, a.shape, mybir.dt.from_np(a.dtype), kind="ExternalInput").ap()
         for n, a in data.items()}
    t["out"] = nc.dram_tensor("out", (B * S, D), F32, kind="ExternalOutput").ap()
    build(nc, t)
    r = run_bass_kernel_spmd(nc, [data], core_ids=[0])
    return r.results[0]["out"].reshape(B, S, D)
```

```python
from contextlib import ExitStack

import concourse.bass as bass
from concourse import mybir

F32 = mybir.dt.float32
BF16 = mybir.dt.bfloat16
I32 = mybir.dt.int32
ALU = mybir.AluOpType
ACT = mybir.ActivationFunctionType
AX_X = mybir.AxisListType.X

P = 128
B, S, D = 64, 128, 256
C = D // P
L, H, DFF = 3, 8, 1024
DK = D // H
FC = DFF // P
XH = 16
XDK = D // XH
G = 2
GROUPS = B // G
T = G * S
UH = 8
UW = UH * S
BANK = 512
FIRST_KEY_MASK = [1, 1, 0]
FFN_LAYERS = [0, 2]
EPS = 1e-5
MASKED = -1e30
ROOT_FLOOR = 1e-19
SCALE = DK ** -0.5
XSCALE = XDK ** -0.5
PAD_BIAS = 1e10 / XSCALE
SEED = 1

TENSOR = [(0, ("k", 0, 0)), (0, ("k", 0, 1)), (1, ("kx", 1)), (1, ("vx", 1)), (1, ("v", 2, 0)), (0, ("v", 0, 1)),
    (0, ("k", 1, 0)), (0, ("scores", (0, 0))), (1, ("pt", (2, 0), 0)), (1, ("v", 2, 1)), (1, ("pt", (2, 0), 1)),
    (1, ("pt", (2, 1), 0)), (1, ("att", (2, 0))), (0, ("scores", (0, 1))), (1, ("o", (2, 0))),
    (1, ("pt", (2, 1), 1)), (1, ("att", (2, 1))), (0, ("k", 1, 1)), (1, ("o", (2, 1))), (0, ("v", 0, 0)),
    (1, ("vx", 0)), (1, ("turn", (2, 1, 0))), (0, ("v", 1, 0)), (1, ("turn", (2, 1, 1))), (1, ("up", 2, 1)),
    (1, ("up", 2, 5)), (1, ("up", 2, 7)), (1, ("up", 2, 0)), (1, ("up", 2, 2)), (0, ("scores", (1, 0))),
    (0, ("scores", (1, 1))), (1, ("up", 2, 4)), (1, ("up", 2, 6)), (1, ("up", 2, 3)), (0, ("pt", (0, 0), 0)),
    (0, ("pt", (0, 0), 1)), (1, ("down", 2, 0)), (0, ("pt", (0, 1), 0)), (0, ("pt", (0, 1), 1)), (1, ("down", 2, 1)),
    (0, ("v", 1, 1)), (0, ("att", (0, 0))), (0, ("att", (0, 1))), (1, ("turn", (2, 2, 0))), (0, ("o", (0, 0))),
    (1, ("turn", (2, 2, 1))), (0, ("o", (0, 1))), (1, ("q", 0)), (1, ("q", 1)), (1, ("scores", (3, 0, 0))),
    (0, ("pt", (1, 0), 0)), (0, ("pt", (1, 0), 1)), (1, ("scores", (3, 0, 1))), (0, ("att", (1, 0))),
    (0, ("pt", (1, 1), 0)), (0, ("turn", (0, 1, 0))), (0, ("turn", (0, 1, 1))), (0, ("o", (1, 0))),
    (0, ("pt", (1, 1), 1)), (0, ("up", 0, 7)), (0, ("up", 0, 4)), (0, ("att", (1, 1))), (1, ("pt", (3, 0, 0), 0)),
    (0, ("up", 0, 1)), (0, ("o", (1, 1))), (1, ("scores", (3, 1, 0))), (1, ("pt", (3, 0, 1), 0)), (0, ("up", 0, 2)),
    (0, ("up", 0, 0)), (0, ("up", 0, 3)), (1, ("pt", (3, 0, 1), 1)), (1, ("scores", (3, 1, 1))),
    (0, ("turn", (1, 1, 1))), (0, ("turn", (1, 1, 0))), (0, ("up", 0, 6)), (0, ("k", 2, 1)), (0, ("k", 2, 0)),
    (0, ("up", 0, 5)), (0, ("down", 0, 1)), (1, ("pt", (3, 0, 0), 1)), (0, ("down", 0, 0)), (0, ("scores", (2, 0))),
    (1, ("att", (3, 0, 0))), (0, ("scores", (2, 1))), (1, ("pt", (3, 1, 0), 0)), (1, ("pt", (3, 1, 0), 1)),
    (1, ("att", (3, 0, 1))), (1, ("pt", (3, 1, 1), 0)), (1, ("o", (3, 0, 1))), (1, ("pt", (3, 1, 1), 1)),
    (1, ("att", (3, 1, 0))), (0, ("turn", (0, 2, 1))), (1, ("att", (3, 1, 1))), (0, ("kx", 0)),
    (1, ("o", (3, 1, 1))), (0, ("turn", (0, 2, 0)))]
SCALAR = [(0, ("k", 0, 0)), (0, ("k", 0, 1)), (1, ("effect", (2, 1))), (1, ("exp2", (2, 0))), (1, ("v", 2, 0)),
    (1, ("exp2", (2, 1))), (0, ("exp1", (0, 0))), (1, ("v", 2, 1)), (1, ("pt", (2, 1), 0)), (1, ("att", (2, 0))),
    (0, ("effect", (0, 0))), (1, ("att", (2, 1))), (0, ("k", 1, 1)), (0, ("exp1", (0, 1))), (1, ("vx", 0)),
    (0, ("v", 0, 0)), (1, ("turn", (2, 1, 0))), (0, ("v", 1, 0)), (1, ("turn", (2, 1, 1))), (1, ("up", 2, 1)),
    (0, ("effect", (0, 1))), (0, ("exp2", (0, 0))), (0, ("exp1", (1, 0))), (1, ("up", 2, 4)), (1, ("up", 2, 3)),
    (1, ("up", 2, 6)), (0, ("exp2", (0, 1))), (0, ("pt", (0, 0), 1)), (0, ("exp1", (1, 1))), (0, ("effect", (1, 0))),
    (0, ("pt", (0, 1), 1)), (0, ("pt", (0, 1), 0)), (0, ("effect", (1, 1))), (0, ("v", 1, 1)), (0, ("att", (0, 1))),
    (1, ("turn", (2, 2, 0))), (0, ("exp2", (1, 0))), (1, ("q", 0)), (0, ("exp2", (1, 1))), (0, ("pt", (1, 0), 1)),
    (1, ("exp1", (3, 0, 0))), (0, ("turn", (0, 1, 0))), (0, ("turn", (0, 1, 1))), (0, ("up", 0, 7)),
    (0, ("up", 0, 4)), (1, ("exp1", (3, 0, 1))), (1, ("pt", (3, 0, 1), 1)), (0, ("turn", (1, 1, 1))),
    (0, ("turn", (1, 1, 0))), (0, ("up", 0, 6)), (0, ("k", 2, 1)), (0, ("up", 0, 5)), (1, ("exp1", (3, 1, 1))),
    (1, ("pt", (3, 0, 0), 1)), (1, ("exp1", (3, 1, 0))), (0, ("exp1", (2, 0))), (1, ("pt", (3, 1, 0), 0)),
    (1, ("pt", (3, 1, 0), 1)), (1, ("att", (3, 0, 1))), (0, ("exp1", (2, 1))), (1, ("pt", (3, 1, 1), 1)),
    (1, ("pt", (3, 1, 1), 0)), (0, ("turn", (0, 2, 1))), (1, ("att", (3, 1, 0))), (0, ("effect", (2, 0))),
    (0, ("turn", (0, 2, 0)))]
VECTOR = [(0, ("k", 1, 0)), (0, ("v", 0, 1)), (1, ("max2", (2, 1))), (1, ("prob", (2, 0))), (0, ("max1", (0, 0))),
    (1, ("prob", (2, 1))), (1, ("pt", (2, 0), 0)), (1, ("pt", (2, 0), 1)), (0, ("dist", (0, 0))),
    (0, ("max1", (0, 1))), (1, ("pt", (2, 1), 1)), (1, ("sums", (2, 1, 0))), (0, ("scores2", (0, 0))),
    (1, ("tok", (2, 1, 0))), (1, ("sums", (2, 1, 1))), (1, ("tok", (2, 1, 1))), (0, ("dist", (0, 1))),
    (1, ("up", 2, 5)), (0, ("max2", (0, 0))), (1, ("up", 2, 2)), (1, ("up", 2, 7)), (1, ("up", 2, 0)),
    (0, ("scores2", (0, 1))), (0, ("max1", (1, 0))), (0, ("max2", (0, 1))), (0, ("prob", (0, 0))),
    (0, ("max1", (1, 1))), (0, ("dist", (1, 0))), (0, ("prob", (0, 1))), (0, ("pt", (0, 0), 0)),
    (1, ("sums", (2, 2, 0))), (0, ("dist", (1, 1))), (1, ("sums", (2, 2, 1))), (0, ("scores2", (1, 0))),
    (1, ("tok", (2, 2, 0))), (0, ("att", (0, 0))), (1, ("tok", (2, 2, 1))), (0, ("max2", (1, 0))),
    (0, ("scores2", (1, 1))), (1, ("turn", (2, 2, 1))), (0, ("sums", (0, 1, 0))), (0, ("max2", (1, 1))),
    (0, ("prob", (1, 0))), (0, ("sums", (0, 1, 1))), (1, ("q", 1)), (0, ("pt", (1, 0), 0)), (0, ("prob", (1, 1))),
    (1, ("max1", (3, 0, 0))), (0, ("tok", (0, 1, 0))), (0, ("tok", (0, 1, 1))), (1, ("max1", (3, 0, 1))),
    (0, ("att", (1, 0))), (0, ("pt", (1, 1), 0)), (0, ("pt", (1, 1), 1)), (0, ("sums", (1, 1, 0))),
    (1, ("prob", (3, 0, 0))), (0, ("att", (1, 1))), (1, ("prob", (3, 0, 1))), (1, ("pt", (3, 0, 0), 0)),
    (0, ("up", 0, 1)), (0, ("sums", (1, 1, 1))), (0, ("tok", (1, 1, 1))), (1, ("pt", (3, 0, 1), 0)),
    (0, ("up", 0, 0)), (0, ("up", 0, 2)), (0, ("tok", (1, 1, 0))), (0, ("up", 0, 3)), (0, ("k", 2, 0)),
    (1, ("max1", (3, 1, 1))), (1, ("max1", (3, 1, 0))), (0, ("sums", (0, 2, 1))), (1, ("prob", (3, 1, 0))),
    (1, ("prob", (3, 1, 1))), (0, ("max1", (2, 0))), (1, ("att", (3, 0, 0))), (0, ("sums", (0, 2, 0))),
    (0, ("max1", (2, 1))), (0, ("dist", (2, 0))), (0, ("tok", (0, 2, 1))), (1, ("sums", (3, 1, 0))),
    (0, ("dist", (2, 1))), (1, ("att", (3, 1, 1))), (0, ("tok", (0, 2, 0))), (0, ("kx", 0)), (1, ("tok", (3, 1, 0))),
    (1, ("sums", (3, 1, 1))), (1, ("tok", (3, 1, 1))), (0, ("scores2", (2, 0))), (0, ("kx", 1)),
    (0, ("max2", (2, 0))), (0, ("scores2", (2, 1))), (0, ("vx", 1))]
POOL = [(1, ("select", (2, 0))), (1, ("select", (2, 1))), (1, ("dev", (2, 1, 0))), (1, ("dev", (2, 1, 1))),
    (0, ("select", (0, 0))), (0, ("select", (0, 1))), (1, ("dev", (2, 2, 0))), (1, ("dev", (2, 2, 1))),
    (0, ("select", (1, 0))), (0, ("select", (1, 1))), (0, ("dev", (0, 1, 1))), (0, ("dev", (0, 1, 0))),
    (0, ("dev", (1, 1, 1))), (0, ("dev", (1, 1, 0))), (0, ("dev", (0, 2, 1))), (1, ("dev", (3, 1, 0))),
    (0, ("dev", (0, 2, 0))), (1, ("dev", (3, 1, 1)))]
SYNC = [(0, ("diag", (0, 0))), (0, ("diag", (0, 1))), (0, ("diag", (1, 0))), (0, ("diag", (1, 1))),
    (1, ("diag", (3, 0, 1))), (0, ("load", "x_t")), (1, ("diag", (3, 0, 0))), (1, ("diag", (3, 1, 0))),
    (-1, ("load", "ctx_t")), (1, ("diag", (3, 1, 1))), (-1, ("load", "ctx_f")), (0, ("load", "pad_bias")),
    (0, ("load", "pad_mask")), (0, ("diag", (2, 0))), (0, ("diag", (2, 1))), (0, ("load", "cx_f")),
    (1, ("store", 0)), (-1, ("load", "x_f")), (1, ("store", 1))]

GENERAL_KINDS = ("pt", "att", "o", "turn", "k", "v", "kx", "vx", "q", "up", "down")


def is_layer(u):
    return u[0] < L


def out_key(u):
    return (u[0], 1, u[1])


class Now:

    def __init__(self, it):
        self.it = it
        self.static = isinstance(it, int)

    def steps(self, table):
        return [(self.it - d, d, step) for d, step in table if not self.static or 0 <= self.it - d < GROUPS]


class Order:

    def __init__(self, table, chosen):
        self.events = [(d, step) for d, step in table if chosen(step)]
        self.index = {key: i for i, (_, key) in enumerate(self.events)}
        self.late = {key: d for d, key in self.events}
        assert len(self.index) == len(self.events)

    def _before_turn(self, it):
        return sum(0 <= i - d < GROUPS for i in range(-1, it) for d, _ in self.events)

    def _count(self, now, d, key, back, past):
        it = now.it - d + self.late[key] - back
        i = self.index[key] + past
        if now.static:
            return self._before_turn(it) + sum(0 <= it - e < GROUPS for e, _ in self.events[:i]) + SEED
        return self._before_turn(1) + (it - 1) * len(self.events) + i + SEED

    def upto(self, now, d, key, back=0):
        return self._count(now, d, key, back, 1)

    def before(self, now, d, key):
        return self._count(now, d, key, 0, 0)

    def last(self, key, n=1):
        i = self.index[key] - n
        d, other = self.events[i]
        return d + (i < 0) - self.late[key], other


def kind_order(table, *kinds, chosen=lambda step: True):
    return Order(table, lambda step: step[0] in kinds and chosen(step))


def layer_step(step):
    return is_layer(step[1])


scores_order = kind_order(TENSOR, "scores")
PARITY = {step[1]: i % 2 for i, (_, step) in enumerate(scores_order.events)}
assert len(PARITY) % 2 == 0
bank_order = [kind_order(TENSOR, "scores", chosen=lambda step, p=p: PARITY[step[1]] == p) for p in range(2)]
diag_order = [kind_order(SYNC, "diag", chosen=lambda step, p=p: PARITY[step[1]] == p and layer_step(step))
              for p in range(2)]
xdiag_order = [kind_order(SYNC, "diag", chosen=lambda step, p=p: PARITY[step[1]] == p and not layer_step(step))
               for p in range(2)]
max1_order, dist_order, max2_order, prob_order, sums_order, tok_order = (
    kind_order(VECTOR, kind) for kind in ("max1", "dist", "max2", "prob", "sums", "tok"))
fixed_order = kind_order(VECTOR, "prob", chosen=lambda step: step[1][0] == 2)
exp1_order = kind_order(SCALAR, "exp1", chosen=layer_step)
effect_order, exp2_order = (kind_order(SCALAR, kind) for kind in ("effect", "exp2"))
select_order, dev_order = (kind_order(POOL, kind) for kind in ("select", "dev"))
GEN_BANKS = 4
GEN_BANK = {step: i % GEN_BANKS for i, (_, step) in enumerate(kind_order(TENSOR, *GENERAL_KINDS).events)}
gen_order = [kind_order(TENSOR, *GENERAL_KINDS, chosen=lambda step, i=i: GEN_BANK[step] == i)
             for i in range(GEN_BANKS)]
NORM_SLOT = {step[1]: i % 2 for i, (_, step) in enumerate(sums_order.events)}
assert len(NORM_SLOT) % 2 == 0


def place(table, step):
    return next(d * len(table) + i for i, (d, other) in enumerate(table) if other == step)


def check_reuse():
    rules = []
    for b in range(G):
        for c in range(C):
            rules += [(TENSOR, ("scores", (l, b)), ("k", m, c), back) for l, m, back in ((0, 2, 0), (2, 0, 1), (1, 1, 1))]
            rules += [(TENSOR, ("scores", (3, b, h)), ("kx", c), 1) for h in range(2)]
            rules += [(TENSOR, ("scores", (3, b, c)), ("q", c), 1), (TENSOR, ("att", (3, b, c)), ("vx", b), 1)]
            rules += [(TENSOR, ("k", 2, c), ("turn", (2, 2, b)), 0), (TENSOR, ("q", c), ("turn", (1, 1, b)), 1)]
            rules += [(TENSOR, ("o", (3, b, C - 1)), ("att", (3, b, c)), 1)]
        rules += [(TENSOR, ("att", (l, b)), ("v", m, b), back) for l, m, back in ((0, 0, 1), (1, 2, 0), (2, 1, 1))]
        rules += [(TENSOR, ("o", (l, b)), ("att", (m, b)), back) for l, m, back in ((0, 1, 0), (1, 2, 0), (2, 0, 1))]
        rules += [(TENSOR, ("v", 2, b), ("turn", (2, 1, b)), 0), (TENSOR, ("turn", (0, 2, b)), ("down", 0, b), 1)]
        for f in range(FC):
            rules += [(TENSOR, ("up", 0, f), ("turn", (0, 2, b)), 0), (TENSOR, ("up", 2, f), ("turn", (0, 1, b)), 1)]
            rules += [(TENSOR, ("down", 0, b), ("up", 2, f), 0), (TENSOR, ("down", 2, b), ("up", 0, f), 1)]
        rules += [(VECTOR, ("sums", (2, 2, b)), ("tok", (0, 1, b)), 1), (VECTOR, ("sums", (0, 2, b)), ("tok", (2, 1, b)), 0),
                  (VECTOR, ("sums", (2, 1, b)), ("tok", (1, 1, b)), 1), (VECTOR, ("sums", (3, 1, b)), ("tok", (2, 2, b)), 1)]
    rules += [(TENSOR, ("pt", u, 0), ("pt", u, 1), 0) for u in PARITY]
    for p in range(2):
        for _, step in bank_order[p].events:
            back, other = bank_order[p].last(step)
            rules += [(TENSOR, ("att", other[1]), ("pt", step[1], half), back) for half in range(2)]
    for _, step in sums_order.events:
        back, other = sums_order.last(step, 2)
        rules.append((VECTOR, ("tok", other[1]), step, back))
    for table, reader, refill, back in rules:
        assert place(table, reader) - back * len(table) < place(table, refill), (reader, refill, back)


check_reuse()

BEFORE = [-1, 0, 1]
LOOP = (2, GROUPS - 1)
AFTER = [GROUPS - 1, GROUPS]


def run_turns(eng, turn_of):
    for it in BEFORE:
        turn_of(Now(it))
    with eng.Fori(*LOOP) as it:
        turn_of(Now(it))
    for it in AFTER:
        turn_of(Now(it))


def build(nc, t):
    pad_parts_dram = nc.dram_tensor("pad_parts", (3, B * S), BF16, kind="Internal").ap()
    dam_rows_dram = nc.dram_tensor("dam_rows", (L * H, P, 2 * S), BF16, kind="Internal").ap()

    with ExitStack() as ctx:
        def sb(name, shape, dt=F32):
            return ctx.enter_context(nc.sbuf_tensor(name, shape, dt))

        def sem(name):
            return ctx.enter_context(nc.semaphore(name))

        k_w = [sb(f"k_w{l}", [P, C, D]) for l in range(L)]
        v_w = [sb(f"v_w{l}", [P, C, D]) for l in range(L)]
        o_w = [sb(f"o_w{l}", [P, C, D]) for l in range(L)]
        up_w = {l: sb(f"up_w{l}", [P, C, DFF]) for l in FFN_LAYERS}
        down_w = {l: sb(f"down_w{l}", [P, FC, D]) for l in FFN_LAYERS}
        xq_w, xk_w, xv_w, xo_w = (sb(n, [P, C, D]) for n in ("xq_w", "xk_w", "xv_w", "xo_w"))
        k_bias = sb("k_bias", [P, L, C])
        up_bias = sb("up_bias", [P, 2, FC])
        norm_g = sb("norm_g", [P, 6, D])
        norm_b = sb("norm_b", [P, 6, D])
        ROWS = 9
        row_bias = sb("row_bias", [3, ROWS, D], BF16)
        ident = sb("ident", [P, P])
        ident_bf = sb("ident_bf", [P, P], BF16)
        ones3 = sb("ones3", [3, P], BF16)
        dam_bias = [sb(f"dam_bias{l}", [P, UH, S], BF16) for l in range(L)]
        chain = {m: sb(f"chain{m}", [P, UW], BF16) for m in (0, 1)}
        root_floor = sb("root_floor", [P, 1])
        neg_half = sb("neg_half", [P, 1])
        keep_row = sb("keep_row", [P, 1])
        first_row = sb("first_row", [P, 1])
        ctx_f = sb("ctx_f", [P, C, T])
        x_f = sb("x_f", [P, C, T])
        cx_f = sb("cx_f", [P, C, T])
        ctx_t = sb("ctx_t", [P, G, D])
        x_t = sb("x_t", [P, G, D])
        pad_mask = sb("pad_mask", [P, T])
        pad_bias = sb("pad_bias", [3, T], BF16)
        k_f = [sb(f"k_f{i}", [P, C, T]) for i in range(2)]
        xk_f = sb("xk_f", [P, C, T])
        v_t = [sb(f"v_t{i}", [P, G, D]) for i in range(2)]
        xv_t = sb("xv_t", [P, G, XH // 2, 2, 2, XDK])
        k_diag = sb("k_diag", [P, 2, UW])
        xk_diag = sb("xk_diag", [P, 2, UW])
        E = sb("E", [P, UW])
        suffix = sb("suffix", [P, UW + 1])
        X = sb("X", [P, 2, UW])
        probs_f = sb("probs_f", [P, 2, UW])
        att_f = sb("att_f", [P, G, C, S])
        xatt_f = sb("xatt_f", [P, G, C, S])
        f_buf = sb("f_buf", [P, C, T])
        h_buf = sb("h_buf", [P, C, T])
        q_f = sb("q_f", [P, C, T])
        a_tok = sb("a_tok", [P, G, D])
        x1_tok = sb("x1_tok", [P, G, D])
        x2_tok = sb("x2_tok", [P, G, D])
        y_tok = sb("y_tok", [P, 2, D])
        hidden = sb("hidden", [P, FC, 2 * S])
        out_t = sb("out_t", [P, 2, D])
        res = sb("res", [P, 2, D])
        stats = sb("stats", [P, 2, 6])
        moments = sb("moments", [P, 2, 2])
        rstd = sb("rstd", [P, 2, 1])
        iota_i = sb("iota_i", [P, S], I32)
        pos_f = sb("pos_f", [P, 3, S])
        gam = sb("gam", [P, 4, L * H])
        work = hidden[:, :, :].rearrange("p f n -> p (f n)")
        logits = work[0:L * H, 0:256].rearrange("p (s e) -> p s e", e=2)
        gumbel = work[0:L * H, 256:512].rearrange("p (s e) -> p s e", e=2)
        rows = work[0:ROWS, 512:768]
        rows_parts = work[0:ROWS, 768:1152].bitcast(BF16).rearrange("p (i n) -> p i n", i=3)
        pads = work[0:B, 1152:1280]
        pads_parts = work[0:B, 1280:1472].bitcast(BF16).rearrange("p (i n) -> p i n", i=3)
        dam_rows = work[0:L * H, 1472:1600].bitcast(BF16)
        one_col = sb("one_col", [P, 1])
        eps_col = sb("eps_col", [P, 1])
        m1 = sb("m1", [P, 2, UH])
        nm1 = sb("nm1", [P, 2, UH])
        z1 = sb("z1", [P, 2, UH])
        rz1 = sb("rz1", [P, 2, UH])
        m2 = sb("m2", [P, 2, UH])
        nm2 = sb("nm2", [P, 2, UH])
        z2 = sb("z2", [P, 2, UH])
        rz2 = sb("rz2", [P, 2, UH])

        scores_ps = [ctx.enter_context(nc.psum_tensor(f"scores_ps{i}", [P, UW], F32)) for i in range(2)]
        gen_ps = [ctx.enter_context(nc.psum_tensor(f"gen_ps{i}", [P, BANK], F32)) for i in range(GEN_BANKS)]

        weights_in, setup_in, parts_out, toeplitz_in = (
            sem(n) for n in ("weights_in", "setup_in", "parts_out", "toeplitz_in"))
        pool_step, pool_ready, dve_step, gamma_ready, parts_ready, dve_ready, act_step = (
            sem(n) for n in ("pool_step", "pool_ready", "dve_step", "gamma_ready", "parts_ready", "dve_ready",
                             "act_step"))
        iota_ready, pos_ready, masks_ready = (sem(n) for n in ("iota_ready", "pos_ready", "masks_ready"))
        loaded = {n: sem(f"{n}_in") for n in ("ctx_f", "x_f", "cx_f", "ctx_t", "x_t", "pad_mask", "pad_bias")}
        gen_full = [sem(f"gen_full{i}") for i in range(GEN_BANKS)]
        gen_free = [sem(f"gen_free{i}") for i in range(GEN_BANKS)]
        diag_in = [sem(f"diag_in{i}") for i in range(2)]
        xdiag_in = [sem(f"xdiag_in{i}") for i in range(2)]
        scores_done = sem("scores_done")
        scores_free = [sem(f"scores_free{i}") for i in range(2)]
        max1_done, nm1_done, exp1_done, scan_done, recip_done, rz1_done, x_done = (
            sem(n) for n in ("max1_done", "nm1_done", "exp1_done", "scan_done", "recip_done", "rz1_done", "x_done"))
        ln_done, root_done, te_done, select_done, max2_done, nm2_done, exp2_done = (
            sem(n) for n in ("ln_done", "root_done", "te_done", "select_done", "max2_done", "nm2_done", "exp2_done"))
        z2_fixed, rz2_done, norm_done = (sem(n) for n in ("z2_fixed", "rz2_done", "norm_done"))
        stats_done, moments_done, var_done, rstd_done, scaled_done, tok_done = (
            sem(n) for n in ("stats_done", "moments_done", "var_done", "rstd_done", "scaled_done", "tok_done"))
        passed = sem("passed")
        out_done = [sem(f"out_done{i}") for i in range(2)]
        SETUP_LOADS = 16 * (1 + 2 + ROWS + 1)
        PARTS_OUT = 16 * 7

        def norm_row(key):
            l, which, _ = key
            return 5 if l == 3 else (l if which == 1 else 3 + FFN_LAYERS.index(l))

        def residual(key):
            l, which, b = key
            if which == 2:
                return a_tok[:, b, :]
            return (ctx_t, x_t, x1_tok, x2_tok)[l][:, b, :]

        def norm_out(key):
            l, which, b = key
            if l == 3:
                return out_t[:, b, :]
            if which == 1:
                return (a_tok, x1_tok, a_tok)[l][:, b, :]
            return y_tok[:, b, :] if l == 0 else x2_tok[:, b, :]

        def turn_out(key):
            l, which, b = key
            buf = h_buf if (l == 1 or (l == 2 and which == 2)) else f_buf
            return buf[:, :, b * S:(b + 1) * S]

        def values(l):
            return v_t[0 if l == 0 else 1]

        def wait_apart(eng, sem_, value):
            eng.wait_ge(sem_, value)
            eng.sem_inc(passed, 1)

        def read_out(eng, now, d, *steps, back=0, apart=False):
            for i in range(GEN_BANKS):
                order = gen_order[i]
                mine = [step for step in steps if GEN_BANK[step] == i]
                if mine:
                    last = max(mine, key=lambda step: (order.late[step], order.index[step]))
                    eng.wait_ge(gen_free[i], order.upto(now, d, last, back))
                    if apart:
                        eng.sem_inc(passed, 1)

        def take(eng, now, d, step):
            i = GEN_BANK[step]
            eng.wait_ge(gen_full[i], gen_order[i].upto(now, d, step))
            return gen_ps[i], gen_free[i]

        def wait_turned(eng, now, d, u):
            back, (_, last) = bank_order[PARITY[u]].last(("scores", u))
            i = GEN_BANK["pt", last, 1]
            eng.wait_ge(gen_full[i], gen_order[i].upto(now, d, ("pt", last, 1), back))

        def unit_heads(ap):
            return ap.rearrange("p (h k) -> p h k", k=S)

        def read(eng, vector, now, g, d, step):
            if step[0] == "kx":
                eng.wait_ge(loaded["pad_mask"], 16 * (g + 1))
            ps, free = take(eng, now, d, step)
            copy = nc.vector.tensor_copy if vector else nc.scalar.copy
            kind = step[0]
            if kind == "pt":
                _, u, half = step
                last = copy(probs_f[:, PARITY[u], half * BANK:(half + 1) * BANK], ps[:, :])
            elif kind == "att":
                u = step[1]
                if is_layer(u):
                    last = copy(att_f[:, u[1], :, :].rearrange("p c s -> p (c s)"), ps[:, 0:C * S])
                else:
                    last = copy(xatt_f[:, u[1], u[2], :], ps[:, 0:S])
            elif kind == "turn":
                last = copy(turn_out(step[1]), ps[:, 0:C * S].rearrange("p (c s) -> p c s", c=C))
            elif kind == "k":
                _, l, c = step
                dst, bias = k_f[l % 2][:, c, :], k_bias[:, l, c:c + 1]
                if vector:
                    last = nc.vector.tensor_scalar(dst, ps[:, 0:T], bias, None, ALU.add)
                else:
                    last = nc.scalar.activation(dst, ps[:, 0:T], ACT.Identity, bias=bias)
            elif kind == "v":
                last = copy(values(step[1])[:, step[2], :], ps[:, 0:D])
            elif kind == "kx":
                last = nc.vector.tensor_tensor(xk_f[:, step[1], :], ps[:, 0:T], pad_mask[:, :], ALU.mult)
            elif kind == "vx":
                heads = ps[:, 0:D].rearrange("p (q e d) -> p q e d", e=2, d=XDK)
                for e in range(2):
                    last = copy(xv_t[:, step[1], :, e, e, :], heads[:, :, e, :])
            elif kind == "q":
                last = copy(q_f[:, step[1], :], ps[:, 0:T])
            else:
                _, l, f = step
                bias = up_bias[:, FFN_LAYERS.index(l), f:f + 1]
                if vector:
                    last = nc.vector.tensor_scalar(hidden[:, f, :], ps[:, 0:T], bias, 0.0, ALU.add, ALU.max)
                else:
                    last = nc.scalar.activation(hidden[:, f, :], ps[:, 0:T], ACT.Relu, bias=bias)
            last.then_inc(free, 1)

        block = ctx.enter_context(nc.Block())

        @block.sync
        def _(sp):
            sp.dma_start(gam[:, 0, :], bass.AP(t["gammas"].tensor, 0, [[0, P], [1, L * H]])).then_inc(setup_in, 16)
            sp.dma_start(logits[:, :, :], t["alphas"].rearrange("l h s e -> (l h) s e")).then_inc(setup_in, 16)
            sp.dma_start(gumbel[:, :, :], t["gumbel"].rearrange("l h s e -> (l h) s e")).then_inc(setup_in, 16)
            for i, src in enumerate([t["vb"][0], t["vb"][1], t["vb"][2], t["ob"][0], t["ob"][1], t["ob"][2],
                                     t["b2"][0], t["b2"][2], t["bo"]]):
                sp.dma_start(rows[i:i + 1, :], src.unsqueeze(0)).then_inc(setup_in, 16)
            sp.dma_start(pads[:, :], t["pad"]).then_inc(setup_in, 16)
            n_w = 0
            for l in range(L):
                for dst, name in ((k_w, "kWT"), (v_w, "vWT"), (o_w, "oWT")):
                    sp.dma_start(dst[l][:, :, :], t[name][l].rearrange("(c p) n -> p c n", p=P)).then_inc(weights_in, 16)
                n_w += 3
            sp.dma_start(k_bias[:, :, :], t["kb"]).then_inc(weights_in, 16)
            sp.dma_start(up_bias[:, :, :], t["b1"]).then_inc(weights_in, 16)
            n_w += 2
            for i, l in enumerate(FFN_LAYERS):
                sp.dma_start(up_w[l][:, :, :], t["w1T"][l].rearrange("(c p) n -> p c n", p=P)).then_inc(weights_in, 16)
                sp.dma_start(down_w[l][:, :, :], t["w2T"][l].rearrange("(c p) n -> p c n", p=P)).then_inc(weights_in, 16)
                n_w += 2
            for dst, name in ((xq_w, "wq"), (xk_w, "wk"), (xv_w, "wv"), (xo_w, "wo")):
                sp.dma_start(dst[:, :, :], t[name].rearrange("(c p) n -> p c n", p=P)).then_inc(weights_in, 16)
                n_w += 1
            for dst, srcs in ((norm_g, [t["ln1_g"][0], t["ln1_g"][1], t["ln1_g"][2], t["ln2_g"][0], t["ln2_g"][2],
                                        t["ln_gamma"]]),
                              (norm_b, [t["ln1_b"][0], t["ln1_b"][1], t["ln1_b"][2], t["ln2_b"][0], t["ln2_b"][2],
                                        t["ln_beta"]])):
                for i, src in enumerate(srcs):
                    sp.dma_start(dst[:, i, :], bass.AP(src.tensor, src.offset, [[0, P], [1, D]])).then_inc(weights_in, 16)
                    n_w += 1
            assert n_w == N_WEIGHTS

            sp.wait_ge(parts_ready, 3)
            for i in range(3):
                sp.dma_start(row_bias[i:i + 1, :, :], rows_parts[:, i, :]).then_inc(parts_out, 16)
                sp.dma_start(pad_parts_dram[i].rearrange("(b s) -> b s", b=B), pads_parts[:, i, :]).then_inc(parts_out, 16)
            sp.dma_start(dam_rows_dram, dam_rows[:, :].unsqueeze(1).to_broadcast([L * H, P, 2 * S])).then_inc(parts_out, 16)
            sp.wait_ge(parts_out, PARTS_OUT)
            for l in range(L):
                src = bass.AP(dam_rows_dram.tensor, l * H * P * 2 * S + S, [[2 * S - 1, P], [P * 2 * S, H], [1, S]])
                sp.dma_start(dam_bias[l][:, :, :], src).then_inc(toeplitz_in, 16)
            sp.wait_ge(masks_ready, 2)

            def diag_blocks(now, d, u):
                b, slot = u[1], PARITY[u]
                kind = ("k", u[0]) if is_layer(u) else ("kx",)
                needs = [kind + (c,) for c in (range(C) if is_layer(u) else u[2:])]
                read_out(sp, now, d, *needs, apart=True)
                order = (diag_order if is_layer(u) else xdiag_order)[slot]
                back, (_, last) = order.last(("diag", u))
                wait_apart(sp, scores_done, scores_order.upto(now, d, ("scores", last), back))
                if is_layer(u):
                    for c in range(C):
                        for j in range(P // DK):
                            rows_j = slice(j * DK, (j + 1) * DK)
                            col = c * BANK + j * S
                            sp.dma_start(k_diag[rows_j, slot, col:col + S],
                                         k_f[u[0] % 2][rows_j, c, b * S:(b + 1) * S]).then_inc(diag_in[slot], 16)
                else:
                    for j in range(UH):
                        rows_j = slice(j * XDK, (j + 1) * XDK)
                        sp.dma_start(xk_diag[rows_j, slot, j * S:(j + 1) * S],
                                     xk_f[rows_j, u[2], b * S:(b + 1) * S]).then_inc(xdiag_in[slot], 16)

            def load(now, g, d, name):
                tok = bass.ds(g * T, T)
                done = loaded[name]
                if name in ("ctx_f", "x_f", "cx_f"):
                    dst, src, readers = {
                        "ctx_f": (ctx_f, "ctxT", [("k", 0, 0), ("k", 0, 1), ("v", 0, 0), ("v", 0, 1)]),
                        "x_f": (x_f, "xT", [("k", 1, 0), ("k", 1, 1), ("v", 1, 0), ("v", 1, 1)]),
                        "cx_f": (cx_f, "ctxT", [("kx", 0), ("kx", 1), ("vx", 0), ("vx", 1)])}[name]
                    read_out(sp, now, d, *readers, back=1, apart=True)
                    sp.dma_start(dst[:, :, :], t[src][:, tok].rearrange("(c p) n -> p c n", p=P)).then_inc(done, 16)
                elif name in ("ctx_t", "x_t"):
                    dst, src, l = (ctx_t, "ctx", 0) if name == "ctx_t" else (x_t, "x", 1)
                    read_out(sp, now, d, *[("o", (l, b)) for b in range(G)], back=1, apart=True)
                    sp.dma_start(dst[:, :, :], t[src][tok, :].rearrange("(b s) d -> s b d", s=S)).then_inc(done, 16)
                elif name == "pad_mask":
                    read_out(sp, now, d, ("kx", 0), ("kx", 1), back=1, apart=True)
                    sp.dma_start(pad_mask[:, :], bass.AP(t["pad"].tensor, g * T, [[0, P], [1, T]])).then_inc(done, 16)
                else:
                    back, last = max((scores_order.late[step] * len(PARITY) + i, step)
                                     for i, (_, step) in enumerate(scores_order.events) if not layer_step(step))
                    wait_apart(sp, scores_done, scores_order.upto(now, d, last, 1))
                    sp.dma_start(pad_bias[:, :], pad_parts_dram[:, tok]).then_inc(done, 16)

            def store(now, g, d, b):
                wait_apart(sp, tok_done, tok_order.upto(now, d, ("tok", (3, 1, b))))
                sp.dma_start(t["out"][bass.ds(g * T + b * S, S), :], out_t[:, b, :]).then_inc(out_done[b], 16)

            def turn_of(now):
                for g, d, step in now.steps(SYNC):
                    if step[0] == "diag":
                        diag_blocks(now, d, step[1])
                    elif step[0] == "load":
                        load(now, g, d, step[1])
                    else:
                        store(now, g, d, step[1])

            run_turns(sp, turn_of)
            for i in range(G):
                sp.wait_ge(out_done[i], 16 * GROUPS + SEED)

        @block.tensor
        def _(pe):
            pe.wait_ge(weights_in, 16 * N_WEIGHTS)
            pe.wait_ge(parts_out, PARTS_OUT)
            pe.wait_ge(dve_ready, 1)
            pe.wait_ge(masks_ready, 2)
            pe.wait_ge(pool_ready, 1)

            def in_sbuf(now, d, step, *needs):
                read_out(pe, now, d, *[need for need in needs if GEN_BANK[need] != GEN_BANK[step]])

            def add_row(out, row):
                return nc.tensor.matmul(out, ones3[:, :], row_bias[:, row, :], start=False, stop=True)

            def feature_major(ps, w, src, c):
                for k in range(C):
                    mm = nc.tensor.matmul(ps[:, 0:T], w[:, k, c * P:(c + 1) * P], src[:, k, :], start=(k == 0),
                                          stop=(k == C - 1))
                return mm

            def token_major(ps, w, src, b, row):
                for k in range(C):
                    mm = nc.tensor.matmul(ps[:, 0:D], src[:, k, b * S:(b + 1) * S], w[:, k, :], start=(k == 0),
                                          stop=(k == C - 1 and row is None))
                return mm if row is None else add_row(ps[:, 0:D], row)

            def scores(now, g, d, u):
                p, b = PARITY[u], u[1]
                out = scores_ps[p]
                pe.wait_ge(scores_free[p], bank_order[p].before(now, d, ("scores", u)))
                if is_layer(u):
                    l = u[0]
                    pe.wait_ge(diag_in[p], (diag_order[p].upto(now, d, ("diag", u)) - SEED) * 16 * UH)
                    for c in range(C):
                        half = slice(c * BANK, (c + 1) * BANK)
                        nc.tensor.matmul(out[:, half], k_f[l % 2][:, c, b * S:(b + 1) * S], k_diag[:, p, half],
                                         start=True, stop=False)
                        mm = nc.tensor.matmul(out[:, half], ident_bf[:, :],
                                              dam_bias[l][:, c * 4:(c + 1) * 4, :].rearrange("p h k -> p (h k)"),
                                              start=False, stop=True)
                else:
                    pe.wait_ge(xdiag_in[p], (xdiag_order[p].upto(now, d, ("diag", u)) - SEED) * 16 * UH)
                    pe.wait_ge(loaded["pad_bias"], 16 * (g + 1))
                    read_out(pe, now, d, ("q", u[2]))
                    for half in range(2):
                        cols = slice(half * BANK, (half + 1) * BANK)
                        nc.tensor.matmul(out[:, cols], q_f[:, u[2], b * S:(b + 1) * S], xk_diag[:, p, cols],
                                         start=True, stop=False)
                        bias = pad_bias[:, b * S:(b + 1) * S].unsqueeze(1).to_broadcast([3, BANK // S, S])
                        mm = nc.tensor.matmul(out[:, cols], ones3[:, :], bias, start=False, stop=True)
                mm.then_inc(scores_done, 1)

            def probs_turn(ps, now, d, u, half):
                pe.wait_ge(norm_done, prob_order.upto(now, d, ("prob", u)))
                for j in range(4):
                    h = half * 4 + j
                    mm = nc.tensor.transpose(ps[:, j * S:(j + 1) * S], X[:, PARITY[u], h * S:(h + 1) * S], ident[:, :])
                return mm

            def attend(ps, now, d, u):
                b = u[1]
                value_step = ("v", u[0], b) if is_layer(u) else ("vx", b)
                for half in range(2):
                    in_sbuf(now, d, ("att", u), ("pt", u, half), *([value_step] if half == 0 else []))
                    for j in range(4):
                        h = half * 4 + j
                        probs = probs_f[:, PARITY[u], h * S:(h + 1) * S]
                        if is_layer(u):
                            mm = nc.tensor.matmul(ps[j * DK:(j + 1) * DK, half * S:(half + 1) * S],
                                                  values(u[0])[:, b, h * DK:(h + 1) * DK], probs, start=True, stop=True)
                        else:
                            pair, e = h // 2, h % 2
                            v = xv_t[:, b, u[2] * 4 + pair, e, :, :].rearrange("p e d -> p (e d)")
                            mm = nc.tensor.matmul(ps[pair * 32:(pair + 1) * 32, 0:S], v, probs,
                                                  start=(e == 0), stop=(e == 1))
                return mm

            def out_proj(ps, now, d, u):
                b = u[1]
                in_sbuf(now, d, ("o", u), *([("att", u)] if is_layer(u) else [("att", (3, b, c)) for c in range(C)]))
                w, att, row = (o_w[u[0]], att_f, 3 + u[0]) if is_layer(u) else (xo_w, xatt_f, 8)
                for c in range(C):
                    nc.tensor.matmul(ps[:, 0:D], att[:, b, c, :], w[:, c, :], start=(c == 0), stop=False)
                return add_row(ps[:, 0:D], row)

            def turn(ps, now, d, key):
                pe.wait_ge(tok_done, tok_order.upto(now, d, ("tok", key)))
                for c in range(C):
                    mm = nc.tensor.transpose(ps[:, c * S:(c + 1) * S], norm_out(key)[:, c * P:(c + 1) * P], ident[:, :])
                return mm

            def project(ps, now, g, d, step):
                kind, i = step[0], step[-1]
                if kind in ("k", "v") and step[1] < 2:
                    pe.wait_ge(loaded[("ctx_f", "x_f")[step[1]]], 16 * (g + 1))
                if kind in ("kx", "vx"):
                    pe.wait_ge(loaded["cx_f"], 16 * (g + 1))
                if kind == "k":
                    l = step[1]
                    if l == 2:
                        in_sbuf(now, d, step, *[("turn", (1, 1, b)) for b in range(G)])
                    return feature_major(ps, k_w[l], (ctx_f, x_f, h_buf)[l], i)
                if kind == "v":
                    l = step[1]
                    if l == 2:
                        in_sbuf(now, d, step, ("turn", (0, 2, i)))
                    return token_major(ps, v_w[l], (ctx_f, x_f, f_buf)[l], i, l)
                if kind == "kx":
                    return feature_major(ps, xk_w, cx_f, i)
                if kind == "vx":
                    return token_major(ps, xv_w, cx_f, i, None)
                in_sbuf(now, d, step, *[("turn", (2, 2, b)) for b in range(G)])
                return feature_major(ps, xq_w, h_buf, i)

            def up(ps, now, d, l, f):
                in_sbuf(now, d, ("up", l, f), *[("turn", (l, 1, b)) for b in range(G)])
                return feature_major(ps, up_w[l], f_buf, f)

            def down(ps, now, d, l, b):
                for f in range(FC):
                    if f % 4 == 0:
                        in_sbuf(now, d, ("down", l, b), *[("up", l, f + i) for i in range(4)])
                    nc.tensor.matmul(ps[:, 0:D], hidden[:, f, b * S:(b + 1) * S], down_w[l][:, f, :],
                                     start=(f == 0), stop=False)
                return add_row(ps[:, 0:D], 6 + FFN_LAYERS.index(l))

            def turn_of(now):
                for g, d, step in now.steps(TENSOR):
                    if step[0] == "scores":
                        scores(now, g, d, step[1])
                        continue
                    i = GEN_BANK[step]
                    pe.wait_ge(gen_free[i], gen_order[i].before(now, d, step))
                    ps = gen_ps[i]
                    if step[0] == "pt":
                        last = probs_turn(ps, now, d, *step[1:])
                    elif step[0] == "att":
                        last = attend(ps, now, d, step[1])
                    elif step[0] == "o":
                        last = out_proj(ps, now, d, step[1])
                    elif step[0] == "turn":
                        last = turn(ps, now, d, step[1])
                    elif step[0] == "up":
                        last = up(ps, now, d, *step[1:])
                    elif step[0] == "down":
                        last = down(ps, now, d, *step[1:])
                    else:
                        last = project(ps, now, g, d, step)
                    last.then_inc(gen_full[i], 1)

            run_turns(pe, turn_of)

        @block.scalar
        def _(act):
            nc.scalar.preload_act_table_set("natural_log_exp_and_others")
            act.wait_ge(pool_ready, 1)
            act.wait_ge(gamma_ready, 1)
            nc.scalar.activation(gam[:, 1, :], gam[:, 1, :], ACT.Exp, scale=-1.0).then_inc(act_step, 1)
            act.wait_ge(act_step, 1)
            nc.scalar.activation(gam[:, 1, :], gam[:, 1, :], ACT.Ln, bias=one_col[:, :]).then_inc(act_step, 1)
            nc.scalar.activation(gumbel[:, :, :], gumbel[:, :, :], ACT.Ln, bias=eps_col[0:L * H, :]).then_inc(act_step, 1)
            act.wait_ge(weights_in, 16 * N_WEIGHTS)
            act.wait_ge(dve_ready, 1)

            def exps(src, minus_max, dst, sums, scale, done):
                for h in range(UH):
                    cols = slice(h * S, (h + 1) * S)
                    a = nc.scalar.activation(dst[:, cols], src[:, cols], ACT.Exp, bias=minus_max[:, h:h + 1], scale=scale,
                                             accum_out=sums[:, h:h + 1])
                a.then_inc(done, 1)

            def scanned(now, d, u):
                back, (_, last) = exp1_order.last(("exp1", u))
                return dist_order.upto(now, d, ("dist", last), back)

            def exp1(now, d, u):
                p = PARITY[u]
                act.wait_ge(nm1_done, max1_order.upto(now, d, ("max1", u)))
                if is_layer(u):
                    act.wait_ge(scan_done, scanned(now, d, u))
                    exps(scores_ps[p], nm1[:, p, :], E[:, :], z1[:, p, :], SCALE, exp1_done)
                else:
                    wait_turned(act, now, d, u)
                    exps(scores_ps[p], nm1[:, p, :], X[:, p, :], z2[:, p, :], XSCALE, scores_free[p])

            def effect(now, d, u):
                n = effect_order.upto(now, d, ("effect", u))
                x = X[:, PARITY[u], :]
                act.wait_ge(x_done, dist_order.upto(now, d, ("dist", u)))
                nc.scalar.activation(x, x, ACT.Ln, bias=root_floor[:, :]).then_inc(ln_done, 1)
                act.wait_ge(ln_done, n)
                nc.scalar.activation(x, x, ACT.Exp, scale=0.5).then_inc(root_done, 1)
                act.wait_ge(root_done, n)
                nc.scalar.activation(x, x, ACT.Exp, scale=-1.0).then_inc(te_done, 1)

            def exp2(now, d, u):
                p = PARITY[u]
                act.wait_ge(nm2_done, max2_order.upto(now, d, ("max2", u)))
                exps(X[:, p, :], nm2[:, p, :], X[:, p, :], z2[:, p, :], SCALE, exp2_done)

            def turn_of(now):
                for g, d, step in now.steps(SCALAR):
                    if step[0] in GENERAL_KINDS:
                        read(act, False, now, g, d, step)
                    else:
                        {"exp1": exp1, "effect": effect, "exp2": exp2}[step[0]](now, d, step[1])

            run_turns(act, turn_of)

        @block.vector
        def _(dve):
            steps = [0]

            def link(ins):
                steps[0] += 1
                ins.then_inc(dve_step, 1)
                dve.wait_ge(dve_step, steps[0])

            dve.wait_ge(setup_in, SETUP_LOADS)
            link(nc.vector.tensor_scalar(gam[:, 3, :], gam[:, 0, :], -1.0, None, ALU.mult))
            link(nc.vector.tensor_scalar(gam[:, 2, :], gam[:, 0, :], 0.0, None, ALU.max))
            nc.vector.tensor_tensor(gam[:, 1, :], gam[:, 0, :], gam[:, 3, :], ALU.max).then_inc(gamma_ready, 1)
            link(nc.vector.tensor_scalar(pads[:, :], pads[:, :], -1.0, PAD_BIAS, ALU.add, ALU.mult))
            for whole, parts in ((pads, pads_parts), (rows, rows_parts)):
                for i in range(3):
                    ins = nc.vector.tensor_copy(parts[:, i, :], whole[:, :])
                    if i < 2:
                        link(ins)
                        link(nc.vector.tensor_tensor(whole[:, :], whole[:, :], parts[:, i, :], ALU.subtract))
                    else:
                        ins.then_inc(parts_ready, 1)
            dve.wait_ge(act_step, 3)
            link(nc.vector.tensor_tensor(logits[:, :, :], logits[:, :, :], gumbel[:, :, :], ALU.subtract))
            link(nc.vector.tensor_tensor(gumbel[:, :, 0], logits[:, :, 0], logits[:, :, 1], ALU.is_ge))
            link(nc.vector.memset(dam_rows[:, 0:S], 0.0))
            link(nc.vector.tensor_scalar(dam_rows[:, S:2 * S], gumbel[:, :, 0], MASKED, None, ALU.mult))
            nc.vector.memset(dam_rows[0:2 * H, S:S + 1], 0.0).then_inc(parts_ready, 1)
            link(nc.vector.tensor_tensor(gam[:, 1, :], gam[:, 1, :], gam[:, 2, :], ALU.add))
            link(nc.vector.tensor_tensor(gam[:, 1, :], gam[:, 1, :], gam[:, 1, :], ALU.mult))
            dve.wait_ge(iota_ready, 1)
            nc.vector.tensor_copy(pos_f[:, 2, :], iota_i[:, :]).then_inc(pos_ready, 1)
            dve.wait_ge(masks_ready, 1)
            for m in (0, 1):
                for h in range(UH):
                    link(nc.vector.tensor_scalar(chain[m][:, h * S:(h + 1) * S], pos_f[:, m, :], 0.0, None, ALU.is_gt))
            link(nc.vector.tensor_copy(ident_bf[:, :], ident[:, :]))
            dve.wait_ge(toeplitz_in, 16 * L)
            nc.vector.memset(dam_bias[2][0:1, :, 0:1], 0.0).then_inc(dve_ready, 1)
            dve.wait_ge(weights_in, 16 * N_WEIGHTS)
            dve.wait_ge(pool_ready, 1)

            def max1(now, d, u):
                p, n = PARITY[u], max1_order.upto(now, d, ("max1", u))
                dve.wait_ge(scores_done, scores_order.upto(now, d, ("scores", u)))
                nc.vector.tensor_reduce(m1[:, p, :], unit_heads(scores_ps[p][:, :]), AX_X, ALU.max).then_inc(max1_done, 1)
                dve.wait_ge(max1_done, n)
                nc.vector.tensor_scalar(nm1[:, p, :], m1[:, p, :], -(SCALE if is_layer(u) else XSCALE), None, ALU.mult
                                        ).then_inc(nm1_done, 1)

            def distance(now, d, u):
                p, l, n = PARITY[u], u[0], dist_order.upto(now, d, ("dist", u))
                dve.wait_ge(exp1_done, exp1_order.upto(now, d, ("exp1", u)))
                nc.vector.reciprocal(rz1[:, p, :], z1[:, p, :]).then_inc(recip_done, 1)
                dve.wait_ge(x_done, dist_order.before(now, d, ("dist", u)))
                nc.vector.tensor_tensor_scan(suffix[:, UW - 1::-1], chain[FIRST_KEY_MASK[l]][:, ::-1], E[:, ::-1], 0.0,
                                             ALU.mult, ALU.add).then_inc(scan_done, 1)
                dve.wait_ge(recip_done, n)
                nc.vector.tensor_tensor(rz1[:, p, :], rz1[:, p, :], gam[:, 1, l * H:(l + 1) * H], ALU.mult
                                        ).then_inc(rz1_done, 1)
                dve.wait_ge(rz1_done, n)
                dve.wait_ge(scan_done, n)
                wait_turned(dve, now, d, u)
                for h in range(UH):
                    ins = nc.vector.scalar_tensor_tensor(out=X[:, p, h * S:(h + 1) * S],
                                                         in0=suffix[:, h * S + 1:(h + 1) * S + 1],
                                                         scalar=rz1[:, p, h:h + 1], in1=pos_f[:, FIRST_KEY_MASK[l], :],
                                                         op0=ALU.mult, op1=ALU.mult)
                ins.then_inc(x_done, 1)

            def scores2(now, d, u):
                p = PARITY[u]
                dve.wait_ge(te_done, effect_order.upto(now, d, ("effect", u)))
                nc.vector.scalar_tensor_tensor(out=X[:, p, :], in0=X[:, p, :], scalar=1e-5, in1=scores_ps[p][:, :],
                                               op0=ALU.max, op1=ALU.mult).then_inc(scores_free[p], 1)

            def max2(now, d, u):
                p, n = PARITY[u], max2_order.upto(now, d, ("max2", u))
                dve.wait_ge(select_done, select_order.upto(now, d, ("select", u)))
                nc.vector.tensor_reduce(m2[:, p, :], unit_heads(X[:, p, :]), AX_X, ALU.max).then_inc(max2_done, 1)
                dve.wait_ge(max2_done, n)
                keep = keep_row[:, 0:1] if u[0] == 2 else 1.0
                nc.vector.tensor_scalar(nm2[:, p, :], m2[:, p, :], -SCALE, keep, ALU.mult, ALU.mult
                                        ).then_inc(nm2_done, 1)

            def normalise(now, d, u):
                p, n = PARITY[u], prob_order.upto(now, d, ("prob", u))
                if is_layer(u):
                    dve.wait_ge(exp2_done, exp2_order.upto(now, d, ("exp2", u)))
                else:
                    dve.wait_ge(scores_free[p], bank_order[p].upto(now, d, ("scores", u)))
                if u[0] == 2:
                    nc.vector.tensor_scalar(z2[:, p, :], z2[:, p, :], first_row[:, 0:1], None, ALU.add
                                            ).then_inc(z2_fixed, 1)
                    dve.wait_ge(z2_fixed, fixed_order.upto(now, d, ("prob", u)))
                nc.vector.reciprocal(rz2[:, p, :], z2[:, p, :]).then_inc(rz2_done, 1)
                dve.wait_ge(rz2_done, n)
                nc.vector.tensor_tensor(unit_heads(X[:, p, :]), unit_heads(X[:, p, :]),
                                        rz2[:, p, :].unsqueeze(2).to_broadcast([P, UH, S]), ALU.mult
                                        ).then_inc(norm_done, 1)

            def norm_sums(now, g, d, key):
                i, n = NORM_SLOT[key], sums_order.upto(now, d, ("sums", key))
                unit = key[::2] if key[0] < 3 else (3, key[2], C - 1)
                step = ("o", unit) if key[1] == 1 else ("down", key[0], key[2])
                back, (_, last) = sums_order.last(("sums", key), 2)
                dve.wait_ge(tok_done, tok_order.upto(now, d, ("tok", last), back))
                ps, free = take(dve, now, d, step)
                if key[1] == 1 and key[0] < 2:
                    dve.wait_ge(loaded[("ctx_t", "x_t")[key[0]]], 16 * (g + 1))
                nc.vector.tensor_tensor(res[:, i, :], ps[:, 0:D], residual(key), ALU.add).then_inc(free, 1)
                read_out(dve, now, d, step)
                nc.vector.bn_stats(stats[:, i, :], res[:, i, :]).then_inc(stats_done, 1)
                wait_apart(dve, stats_done, n)
                nc.vector.bn_aggr(moments[:, i, :], stats[:, i, :]).then_inc(moments_done, 1)
                dve.wait_ge(moments_done, n)
                nc.vector.scalar_tensor_tensor(out=res[:, i, :], in0=res[:, i, :], scalar=moments[:, i, 0:1],
                                               in1=norm_g[:, norm_row(key), :], op0=ALU.subtract, op1=ALU.mult
                                               ).then_inc(scaled_done, 1)

            def norm_tokens(now, g, d, key):
                i = NORM_SLOT[key]
                dve.wait_ge(scaled_done, sums_order.upto(now, d, ("sums", key)))
                dve.wait_ge(rstd_done, dev_order.upto(now, d, ("dev", key)))
                if key[0] == 3:
                    dve.wait_ge(out_done[key[2]], 16 * g + SEED)
                nc.vector.scalar_tensor_tensor(out=norm_out(key), in0=res[:, i, :], scalar=rstd[:, i, 0:1],
                                               in1=norm_b[:, norm_row(key), :], op0=ALU.mult, op1=ALU.add
                                               ).then_inc(tok_done, 1)

            def turn_of(now):
                for g, d, step in now.steps(VECTOR):
                    if step[0] in GENERAL_KINDS:
                        read(dve, True, now, g, d, step)
                    elif step[0] == "sums":
                        norm_sums(now, g, d, step[1])
                    elif step[0] == "tok":
                        norm_tokens(now, g, d, step[1])
                    else:
                        {"max1": max1, "dist": distance, "scores2": scores2, "max2": max2,
                         "prob": normalise}[step[0]](now, d, step[1])

            run_turns(dve, turn_of)

        @block.gpsimd
        def _(pool):
            n_pool = [0]

            def link(ins):
                n_pool[0] += 1
                ins.then_inc(pool_step, 1)
                pool.wait_ge(pool_step, n_pool[0])

            for seeded in (*gen_free, *gen_full, *scores_free, z2_fixed, *out_done, scores_done, max1_done, nm1_done,
                           exp1_done, scan_done, recip_done, rz1_done, x_done, ln_done, root_done, te_done, select_done,
                           max2_done, nm2_done, exp2_done, rz2_done, norm_done, stats_done, moments_done, var_done,
                           rstd_done, scaled_done, tok_done):
                pool.sem_inc(seeded, SEED)
            nc.gpsimd.iota(iota_i[:, :], [[-1, S]], base=0, channel_multiplier=1).then_inc(iota_ready, 1)
            for tile, value in ((root_floor, ROOT_FLOOR), (neg_half, -0.5), (one_col, 1.0), (eps_col, 1e-5),
                                (keep_row, 1.0), (first_row, 0.0), (ident, 0.0), (ones3, 1.0)):
                link(nc.gpsimd.memset(tile[:, :], value))
            link(nc.gpsimd.memset(keep_row[0:1, :], 0.0))
            link(nc.gpsimd.memset(first_row[0:1, :], 1.0))
            link(nc.gpsimd.memset(suffix[:, UW:UW + 1], 0.0))
            link(nc.gpsimd.affine_select(out=ident[:, :], in_=ident[:, :], compare_op=ALU.not_equal, fill=1.0, base=0,
                                         pattern=[[-1, P]], channel_multiplier=1))
            nc.gpsimd.memset(xv_t[:, :, :, :, :, :], 0.0).then_inc(pool_ready, 1)
            pool.wait_ge(pos_ready, 1)
            for m in (0, 1):
                ins = nc.gpsimd.affine_select(out=pos_f[:, m, :], in_=pos_f[:, 2, :], compare_op=ALU.is_gt, fill=0.0,
                                              base=m - 1, pattern=[[-1, S]], channel_multiplier=1)
                if m == 0:
                    link(ins)
            ins.then_inc(masks_ready, 1)
            link(nc.gpsimd.memset(k_diag[:, :, :], 0.0))
            nc.gpsimd.memset(xk_diag[:, :, :], 0.0).then_inc(masks_ready, 1)

            def select(now, d, u):
                p, m = PARITY[u], FIRST_KEY_MASK[u[0]]
                wait_apart(pool, scores_free[p], bank_order[p].upto(now, d, ("scores", u)))
                x = unit_heads(X[:, p, :])
                nc.gpsimd.affine_select(out=x, in_=x, compare_op=ALU.is_gt, fill=MASKED, base=m,
                                        pattern=[[0, UH], [-1, S]], channel_multiplier=1).then_inc(select_done, 1)

            def deviation(now, d, key):
                i, n = NORM_SLOT[key], dev_order.upto(now, d, ("dev", key))
                pool.wait_ge(moments_done, sums_order.upto(now, d, ("sums", key)))
                nc.gpsimd.tensor_tensor(rstd[:, i, :], moments[:, i, 1:2], eps_col[:, :], ALU.add).then_inc(var_done, 1)
                pool.wait_ge(var_done, n)
                nc.gpsimd.tensor_tensor(rstd[:, i, :], rstd[:, i, :], neg_half[:, :], ALU.pow).then_inc(rstd_done, 1)

            def turn_of(now):
                for g, d, step in now.steps(POOL):
                    {"select": select, "dev": deviation}[step[0]](now, d, step[1])

            run_turns(pool, turn_of)


N_WEIGHTS = 3 * L + 2 + 2 * len(FFN_LAYERS) + 4 + 12


def kernel(x, ctx_1024, mask_BxS2_ff1, L0_xattn_kW, L0_xattn_kb, L0_xattn_vW, L0_xattn_vb, L0_xattn_oW, L0_xattn_ob,
           L0_xattn_gammas, L0_xattn_alphas, L0_xattn_ln1_g, L0_xattn_ln1_b, L0_xattn_w1, L0_xattn_b1, L0_xattn_w2,
           L0_xattn_b2, L0_xattn_ln2_g, L0_xattn_ln2_b, L0_xattn_gumbel_E, L1_xattn_wq, L1_xattn_wk, L1_xattn_wv,
           L1_xattn_wo, L1_xattn_bo, L1_xattn_ln_gamma, L1_xattn_ln_beta):
    import numpy as np
    import concourse.bacc as bacc
    from concourse.bass_utils import run_bass_kernel_spmd

    arr = np.ascontiguousarray
    x, c = np.asarray(x), np.asarray(ctx_1024)
    data = {
        "x": arr(x.reshape(B * S, D)), "ctx": arr(c.reshape(B * S, D)),
        "xT": arr(x.reshape(B * S, D).T), "ctxT": arr(c.reshape(B * S, D).T),
        "pad": arr(np.asarray(mask_BxS2_ff1)),
        "kWT": arr(np.asarray(L0_xattn_kW).transpose(0, 2, 1)), "vWT": arr(np.asarray(L0_xattn_vW).transpose(0, 2, 1)),
        "oWT": arr(np.asarray(L0_xattn_oW).transpose(0, 2, 1)), "w1T": arr(np.asarray(L0_xattn_w1).transpose(0, 2, 1)),
        "w2T": arr(np.asarray(L0_xattn_w2).transpose(0, 2, 1)),
        "kb": arr(np.asarray(L0_xattn_kb).reshape(L, C, P).transpose(2, 0, 1)),
        "b1": arr(np.asarray(L0_xattn_b1)[FFN_LAYERS].reshape(2, FC, P).transpose(2, 0, 1)),
        "vb": L0_xattn_vb, "ob": L0_xattn_ob, "b2": L0_xattn_b2,
        "gammas": L0_xattn_gammas, "alphas": L0_xattn_alphas, "gumbel": L0_xattn_gumbel_E,
        "ln1_g": L0_xattn_ln1_g, "ln1_b": L0_xattn_ln1_b, "ln2_g": L0_xattn_ln2_g, "ln2_b": L0_xattn_ln2_b,
        "wq": L1_xattn_wq, "wk": L1_xattn_wk, "wv": L1_xattn_wv, "wo": L1_xattn_wo, "bo": L1_xattn_bo,
        "ln_gamma": L1_xattn_ln_gamma, "ln_beta": L1_xattn_ln_beta,
    }
    data = {f"in_{n}": arr(a) for n, a in data.items()}
    nc = bacc.Bacc("TRN2", target_bir_lowering=False, num_devices=1)
    t = {n[3:]: nc.dram_tensor(n, a.shape, mybir.dt.from_np(a.dtype), kind="ExternalInput").ap()
         for n, a in data.items()}
    t["out"] = nc.dram_tensor("out", (B * S, D), F32, kind="ExternalOutput").ap()
    build(nc, t)
    r = run_bass_kernel_spmd(nc, [data], core_ids=[0])
    return r.results[0]["out"].reshape(B, S, D)
```

```python
from contextlib import ExitStack

import concourse.bass as bass
from concourse import mybir

F32 = mybir.dt.float32
BF16 = mybir.dt.bfloat16
I32 = mybir.dt.int32
ALU = mybir.AluOpType
ACT = mybir.ActivationFunctionType
AX_X = mybir.AxisListType.X

P = 128
B, S, D = 64, 128, 256
C = D // P
L, H, DFF = 3, 8, 1024
DK = D // H
FC = DFF // P
XH = 16
XDK = D // XH
G = 2
GROUPS = B // G
T = G * S
UH = 8
UW = UH * S
BANK = 512
FIRST_KEY_MASK = [1, 1, 0]
FFN_LAYERS = [0, 2]
EPS = 1e-5
MASKED = -1e30
ROOT_FLOOR = 1e-19
SCALE = DK ** -0.5
XSCALE = XDK ** -0.5
PAD_BIAS = 1e10 / XSCALE
SEED = 1

TENSOR = [(0, ("k", 0)), (1, ("kx",)), (2, ("pt", (3, 1, 1), 0)), (2, ("pt", (3, 1, 1), 1)), (1, ("down", 0)),
    (0, ("scores", (0, 0))), (2, ("att", (3, 1, 0))), (0, ("k", 1)), (0, ("scores", (0, 1))), (1, ("turn", 0, 2)),
    (2, ("att", (3, 1, 1))), (1, ("v", 2)), (1, ("pt", (2, 0), 0)), (1, ("pt", (2, 0), 1)), (1, ("pt", (2, 1), 0)),
    (1, ("pt", (2, 1), 1)), (1, ("att", (2, 0))), (0, ("v", 0)), (1, ("att", (2, 1))), (1, ("o", 2)), (2, ("o", 3)),
    (0, ("scores", (1, 0))), (0, ("scores", (1, 1))), (1, ("turn", 2, 1)), (1, ("up", 2, 0)), (1, ("up", 2, 2)),
    (1, ("up", 2, 1)), (1, ("up", 2, 3)), (0, ("pt", (0, 0), 0)), (0, ("pt", (0, 0), 1)), (1, ("down", 2)),
    (0, ("pt", (0, 1), 0)), (0, ("pt", (0, 1), 1)), (0, ("v", 1)), (1, ("vx",)), (1, ("turn", 2, 2)),
    (0, ("att", (0, 0))), (0, ("att", (0, 1))), (1, ("q",)), (0, ("o", 0)), (1, ("scores", (3, 0, 0))),
    (1, ("scores", (3, 0, 1))), (0, ("pt", (1, 0), 0)), (0, ("pt", (1, 0), 1)), (0, ("pt", (1, 1), 0)),
    (0, ("pt", (1, 1), 1)), (0, ("att", (1, 0))), (0, ("att", (1, 1))), (0, ("o", 1)), (0, ("turn", 0, 1)),
    (1, ("scores", (3, 1, 0))), (0, ("up", 0, 0)), (0, ("turn", 1, 1)), (1, ("pt", (3, 0, 0), 0)), (0, ("k", 2)),
    (1, ("pt", (3, 0, 0), 1)), (1, ("scores", (3, 1, 1))), (1, ("pt", (3, 0, 1), 0)), (1, ("pt", (3, 0, 1), 1)),
    (0, ("up", 0, 2)), (0, ("up", 0, 3)), (0, ("up", 0, 1)), (0, ("scores", (2, 0))), (1, ("att", (3, 0, 1))),
    (0, ("scores", (2, 1))), (1, ("att", (3, 0, 0))), (1, ("pt", (3, 1, 0), 0)), (1, ("pt", (3, 1, 0), 1))]
SCALAR = [(2, ("pt", (3, 0, 0), 1)), (2, ("exp1", (3, 1, 0))), (2, ("pt", (3, 0, 1), 0)), (2, ("exp1", (3, 1, 1))),
    (1, ("up", 0, 3)), (1, ("up", 0, 2)), (1, ("up", 0, 1)), (1, ("exp1", (2, 0))), (2, ("att", (3, 0, 1))),
    (2, ("pt", (3, 1, 0), 0)), (2, ("pt", (3, 1, 0), 1)), (1, ("exp1", (2, 1))), (2, ("att", (3, 0, 0))),
    (1, ("effect", (2, 0))), (1, ("effect", (2, 1))), (2, ("pt", (3, 1, 1), 1)), (1, ("exp2", (2, 0))),
    (2, ("att", (3, 1, 0))), (1, ("exp2", (2, 1))), (1, ("turn", 0, 2)), (0, ("k", 1)), (0, ("exp1", (0, 0))),
    (1, ("pt", (2, 0), 0)), (1, ("pt", (2, 1), 0)), (1, ("pt", (2, 1), 1)), (1, ("att", (2, 0))),
    (0, ("exp1", (0, 1))), (1, ("att", (2, 1))), (0, ("effect", (0, 0))), (0, ("effect", (0, 1))), (0, ("v", 0)),
    (1, ("turn", 2, 1)), (0, ("exp2", (0, 0))), (1, ("up", 2, 0)), (1, ("up", 2, 2)), (0, ("exp1", (1, 0))),
    (1, ("up", 2, 3)), (0, ("exp2", (0, 1))), (0, ("exp1", (1, 1))), (0, ("pt", (0, 0), 0)), (0, ("effect", (1, 0))),
    (0, ("effect", (1, 1))), (0, ("pt", (0, 1), 0)), (0, ("pt", (0, 1), 1)), (0, ("v", 1)), (1, ("vx",)),
    (1, ("turn", 2, 2)), (0, ("exp2", (1, 0))), (0, ("exp2", (1, 1))), (0, ("pt", (1, 0), 0)),
    (0, ("pt", (1, 0), 1)), (0, ("pt", (1, 1), 0)), (0, ("pt", (1, 1), 1)), (0, ("att", (1, 0))),
    (0, ("att", (1, 1))), (1, ("exp1", (3, 0, 0))), (0, ("turn", 0, 1)), (1, ("exp1", (3, 0, 1))),
    (0, ("turn", 1, 1)), (0, ("up", 0, 0))]
VECTOR = [(2, ("neg1", (3, 1, 0))), (2, ("recip", (3, 0, 1))), (2, ("prob", (3, 0, 1))), (2, ("max1", (3, 1, 1))),
    (2, ("recip", (3, 1, 0))), (2, ("neg1", (3, 1, 1))), (2, ("pt", (3, 0, 1), 1)), (2, ("prob", (3, 1, 0))),
    (2, ("recip", (3, 1, 1))), (1, ("max1", (2, 0))), (1, ("neg1", (2, 0))), (2, ("prob", (3, 1, 1))),
    (1, ("max1", (2, 1))), (1, ("neg1", (2, 1))), (1, ("dist", (2, 0))), (0, ("k", 0)), (1, ("dist", (2, 1))),
    (1, ("scores2", (2, 0))), (1, ("kx",)), (2, ("pt", (3, 1, 1), 0)), (1, ("max2", (2, 0))),
    (1, ("scores2", (2, 1))), (1, ("neg2", (2, 0))), (1, ("sums", 0, 2)), (1, ("max2", (2, 1))),
    (1, ("neg2", (2, 1))), (1, ("tok", 0, 2)), (1, ("recip", (2, 0))), (0, ("max1", (0, 0))), (1, ("prob", (2, 0))),
    (0, ("neg1", (0, 0))), (0, ("max1", (0, 1))), (1, ("recip", (2, 1))), (2, ("att", (3, 1, 1))),
    (0, ("neg1", (0, 1))), (1, ("prob", (2, 1))), (1, ("v", 2)), (1, ("pt", (2, 0), 1)), (0, ("dist", (0, 0))),
    (0, ("dist", (0, 1))), (0, ("scores2", (0, 0))), (1, ("sums", 2, 1)), (0, ("scores2", (0, 1))),
    (1, ("tok", 2, 1)), (0, ("max2", (0, 0))), (0, ("neg2", (0, 0))), (0, ("max1", (1, 0))), (0, ("neg1", (1, 0))),
    (2, ("sums", 3, 1)), (0, ("max2", (0, 1))), (0, ("max1", (1, 1))), (0, ("neg2", (0, 1))), (0, ("recip", (0, 0))),
    (0, ("neg1", (1, 1))), (0, ("prob", (0, 0))), (1, ("up", 2, 1)), (0, ("dist", (1, 0))), (0, ("recip", (0, 1))),
    (0, ("prob", (0, 1))), (0, ("pt", (0, 0), 1)), (0, ("dist", (1, 1))), (1, ("sums", 2, 2)),
    (0, ("scores2", (1, 0))), (1, ("tok", 2, 2)), (0, ("scores2", (1, 1))), (0, ("max2", (1, 0))),
    (0, ("neg2", (1, 0))), (0, ("att", (0, 1))), (0, ("att", (0, 0))), (0, ("max2", (1, 1))), (1, ("q",)),
    (0, ("neg2", (1, 1))), (2, ("tok", 3, 1)), (0, ("recip", (1, 0))), (0, ("prob", (1, 0))),
    (1, ("max1", (3, 0, 0))), (0, ("recip", (1, 1))), (1, ("neg1", (3, 0, 0))), (0, ("prob", (1, 1))),
    (0, ("sums", 0, 1)), (1, ("max1", (3, 0, 1))), (0, ("tok", 0, 1)), (1, ("neg1", (3, 0, 1))), (0, ("sums", 1, 1)),
    (1, ("recip", (3, 0, 0))), (0, ("tok", 1, 1)), (1, ("prob", (3, 0, 0))), (1, ("max1", (3, 1, 0))), (0, ("k", 2)),
    (1, ("pt", (3, 0, 0), 0))]
POOL = [(1, ("dev", 0, 2)), (0, ("select", (0, 0))), (1, ("dev", 2, 1)), (0, ("select", (0, 1))), (1, ("dev", 2, 2)),
    (0, ("select", (1, 0))), (2, ("dev", 3, 1)), (0, ("select", (1, 1))), (0, ("dev", 0, 1)), (0, ("dev", 1, 1)),
    (0, ("select", (2, 0))), (0, ("select", (2, 1)))]
SYNC = [(0, ("load", "ctx_f")), (0, ("load", "x_f")), (1, ("load", "pad_bias")), (0, ("diag", (0, 0))),
    (0, ("diag", (0, 1))), (0, ("load", "ctx_t")), (1, ("diag", (3, 0, 1))), (0, ("diag", (1, 0))),
    (0, ("load", "pad_mask")), (0, ("diag", (1, 1))), (1, ("diag", (3, 0, 0))), (1, ("diag", (3, 1, 0))),
    (0, ("load", "x_t")), (1, ("diag", (3, 1, 1))), (0, ("load", "cx_f")), (2, ("store",)), (0, ("diag", (2, 0))),
    (0, ("diag", (2, 1)))]

LATEST = max(d for table in (TENSOR, SCALAR, VECTOR, POOL, SYNC) for d, _ in table)
GENERAL_KINDS = ("pt", "att", "o", "turn", "k", "v", "kx", "vx", "q", "up", "down")


def is_layer(u):
    return u[0] < L


class Now:

    def __init__(self, it):
        self.it = it
        self.static = isinstance(it, int)

    def steps(self, table):
        return [(self.it - d, d, step) for d, step in table if not self.static or 0 <= self.it - d < GROUPS]


class Order:

    def __init__(self, table, chosen):
        self.events = [(d, step) for d, step in table if chosen(step)]
        self.index = {key: i for i, (_, key) in enumerate(self.events)}
        self.late = {key: d for d, key in self.events}
        assert len(self.index) == len(self.events)

    def _before_turn(self, it):
        return sum(0 <= i - d < GROUPS for i in range(it) for d, _ in self.events)

    def _count(self, now, d, key, back, past):
        it = now.it - d + self.late[key] - back
        i = self.index[key] + past
        if now.static:
            return self._before_turn(it) + sum(0 <= it - e < GROUPS for e, _ in self.events[:i]) + SEED
        return self._before_turn(LATEST) + (it - LATEST) * len(self.events) + i + SEED

    def upto(self, now, d, key, back=0):
        return self._count(now, d, key, back, 1)

    def before(self, now, d, key):
        return self._count(now, d, key, 0, 0)

    def last(self, key, n=1):
        i = self.index[key] - n
        d, other = self.events[i]
        return d + (i < 0) - self.late[key], other


def kind_order(table, *kinds, chosen=lambda step: True):
    return Order(table, lambda step: step[0] in kinds and chosen(step))


def layer_step(step):
    return is_layer(step[1])


scores_order = kind_order(TENSOR, "scores")
PARITY = {step[1]: i % 2 for i, (_, step) in enumerate(scores_order.events)}
assert len(PARITY) % 2 == 0
bank_order = [kind_order(TENSOR, "scores", chosen=lambda step, p=p: PARITY[step[1]] == p) for p in range(2)]
diag_order = [kind_order(SYNC, "diag", chosen=lambda step, p=p: PARITY[step[1]] == p and layer_step(step))
              for p in range(2)]
xdiag_order = [kind_order(SYNC, "diag", chosen=lambda step, p=p: PARITY[step[1]] == p and not layer_step(step))
               for p in range(2)]
max1_order, neg1_order, dist_order, max2_order, neg2_order, recip_order, prob_order, sums_order, tok_order = (
    kind_order(VECTOR, kind) for kind in ("max1", "neg1", "dist", "max2", "neg2", "recip", "prob", "sums", "tok"))
fixed_order = kind_order(VECTOR, "recip", chosen=lambda step: step[1][0] == 2)
exp1_order = kind_order(SCALAR, "exp1", chosen=layer_step)
effect_order, exp2_order = (kind_order(SCALAR, kind) for kind in ("effect", "exp2"))
select_order, dev_order = (kind_order(POOL, kind) for kind in ("select", "dev"))
GEN_BANKS = 4
GEN_BANK = {step: i % GEN_BANKS for i, (_, step) in enumerate(kind_order(TENSOR, *GENERAL_KINDS).events)}
gen_order = [kind_order(TENSOR, *GENERAL_KINDS, chosen=lambda step, i=i: GEN_BANK[step] == i)
             for i in range(GEN_BANKS)]
NORM_SLOT = {step[1:]: i % 2 for i, (_, step) in enumerate(sums_order.events)}
assert len(NORM_SLOT) % 2 == 0


def place(table, step):
    return next(d * len(table) + i for i, (d, other) in enumerate(table) if other == step)


def check_reuse():
    rules = []
    for b in range(G):
        rules += [(TENSOR, ("scores", (l, b)), ("k", m), back) for l, m, back in ((0, 2, 0), (2, 0, 1), (1, 1, 1))]
        rules += [(TENSOR, ("att", (l, b)), ("v", m), back) for l, m, back in ((0, 0, 1), (1, 2, 0), (2, 1, 1))]
        rules += [(TENSOR, ("o", l), ("att", (m, b)), back) for l, m, back in ((0, 1, 0), (1, 2, 0), (2, 0, 1))]
        for c in range(C):
            rules += [(TENSOR, ("scores", (3, b, c)), (kind,), 1) for kind in ("kx", "q")]
            rules += [(TENSOR, ("att", (3, b, c)), ("vx",), 1), (TENSOR, ("o", 3), ("att", (3, b, c)), 1)]
    rules += [(TENSOR, ("k", 2), ("turn", 2, 2), 0), (TENSOR, ("q",), ("turn", 1, 1), 1)]
    rules += [(TENSOR, ("v", 2), ("turn", 2, 1), 0), (TENSOR, ("turn", 0, 2), ("down", 0), 1)]
    for pair in range(FC // 2):
        rules += [(TENSOR, ("up", 0, pair), ("turn", 0, 2), 0), (TENSOR, ("up", 2, pair), ("turn", 0, 1), 1)]
        rules += [(TENSOR, ("down", 0), ("up", 2, pair), 0), (TENSOR, ("down", 2), ("up", 0, pair), 1)]
    rules += [(VECTOR, ("sums", 2, 2), ("tok", 0, 1), 1), (VECTOR, ("sums", 0, 2), ("tok", 2, 1), 0),
              (VECTOR, ("sums", 2, 1), ("tok", 1, 1), 1), (VECTOR, ("sums", 3, 1), ("tok", 2, 2), 1)]
    rules += [(TENSOR, ("pt", u, 0), ("pt", u, 1), 0) for u in PARITY]
    for p in range(2):
        for _, step in bank_order[p].events:
            back, other = bank_order[p].last(step)
            rules += [(TENSOR, ("att", other[1]), ("pt", step[1], half), back) for half in range(2)]
    for _, step in sums_order.events:
        back, other = sums_order.last(step, 2)
        rules.append((VECTOR, ("tok",) + other[1:], step, back))
    for table, reader, refill, back in rules:
        assert place(table, reader) - back * len(table) < place(table, refill), (reader, refill, back)


check_reuse()

BEFORE = range(LATEST + 1)
LOOP = (LATEST + 1, GROUPS)
AFTER = range(GROUPS, GROUPS + LATEST)


def run_turns(eng, turn_of):
    for it in BEFORE:
        turn_of(Now(it))
    with eng.Fori(*LOOP) as it:
        turn_of(Now(it))
    for it in AFTER:
        turn_of(Now(it))


def build(nc, t):
    pad_parts_dram = nc.dram_tensor("pad_parts", (3, B * S), BF16, kind="Internal").ap()
    dam_rows_dram = nc.dram_tensor("dam_rows", (L * H, P, 2 * S), BF16, kind="Internal").ap()

    with ExitStack() as ctx:
        def sb(name, shape, dt=F32):
            return ctx.enter_context(nc.sbuf_tensor(name, shape, dt))

        def sem(name):
            return ctx.enter_context(nc.semaphore(name))

        k_w = [sb(f"k_w{l}", [P, C, D]) for l in range(L)]
        v_w = [sb(f"v_w{l}", [P, C, D]) for l in range(L)]
        o_w = [sb(f"o_w{l}", [P, C, D]) for l in range(L)]
        up_w = {l: sb(f"up_w{l}", [P, C, DFF]) for l in FFN_LAYERS}
        down_w = {l: sb(f"down_w{l}", [P, FC, D]) for l in FFN_LAYERS}
        xq_w, xk_w, xv_w, xo_w = (sb(n, [P, C, D]) for n in ("xq_w", "xk_w", "xv_w", "xo_w"))
        k_bias = sb("k_bias", [P, L, C])
        up_bias = sb("up_bias", [P, 2, FC])
        norm_g = sb("norm_g", [P, 6, D])
        norm_b = sb("norm_b", [P, 6, D])
        ROWS = 9
        row_bias = sb("row_bias", [3, ROWS, D], BF16)
        ident = sb("ident", [P, P])
        ident_bf = sb("ident_bf", [P, P], BF16)
        ones3 = sb("ones3", [3, P], BF16)
        dam_bias = [sb(f"dam_bias{l}", [P, UH, S], BF16) for l in range(L)]
        chain = {m: sb(f"chain{m}", [P, UW], BF16) for m in (0, 1)}
        root_floor = sb("root_floor", [P, 1])
        neg_half = sb("neg_half", [P, G])
        keep_row = sb("keep_row", [P, 1])
        first_row = sb("first_row", [P, 1])
        ctx_f = sb("ctx_f", [P, C, T])
        x_f = sb("x_f", [P, C, T])
        cx_f = sb("cx_f", [P, C, T])
        ctx_t = sb("ctx_t", [P, G, D])
        x_t = sb("x_t", [P, G, D])
        pad_mask = sb("pad_mask", [P, T])
        pad_bias = sb("pad_bias", [3, T], BF16)
        k_f = [sb(f"k_f{i}", [P, C, T]) for i in range(2)]
        xk_f = sb("xk_f", [P, C, T])
        v_t = [sb(f"v_t{i}", [P, G, D]) for i in range(2)]
        xv_t = sb("xv_t", [P, G, XH // 2, 2, 2, XDK])
        k_diag = sb("k_diag", [P, 2, UW])
        xk_diag = sb("xk_diag", [P, 2, UW])
        E = sb("E", [P, UW])
        suffix = sb("suffix", [P, UW + 1])
        X = sb("X", [P, 2, UW])
        probs_f = sb("probs_f", [P, 2, UW])
        att_f = sb("att_f", [P, G, C, S])
        xatt_f = sb("xatt_f", [P, G, C, S])
        f_buf = sb("f_buf", [P, C, T])
        h_buf = sb("h_buf", [P, C, T])
        q_f = sb("q_f", [P, C, T])
        a_tok = sb("a_tok", [P, G, D])
        x1_tok = sb("x1_tok", [P, G, D])
        x2_tok = sb("x2_tok", [P, G, D])
        y_tok = sb("y_tok", [P, G, D])
        hidden = sb("hidden", [P, FC, 2 * S])
        out_t = sb("out_t", [P, G, D])
        res = sb("res", [P, 2, G, D])
        stats = sb("stats", [P, 2, G, 6])
        moments = sb("moments", [P, 2, G, 2])
        rstd = sb("rstd", [P, 2, G])
        iota_i = sb("iota_i", [P, S], I32)
        pos_f = sb("pos_f", [P, 3, S])
        gam = sb("gam", [P, 4, L * H])
        work = hidden[:, :, :].rearrange("p f n -> p (f n)")
        logits = work[0:L * H, 0:256].rearrange("p (s e) -> p s e", e=2)
        gumbel = work[0:L * H, 256:512].rearrange("p (s e) -> p s e", e=2)
        rows = work[0:ROWS, 512:768]
        rows_parts = work[0:ROWS, 768:1152].bitcast(BF16).rearrange("p (i n) -> p i n", i=3)
        pads = work[0:B, 1152:1280]
        pads_parts = work[0:B, 1280:1472].bitcast(BF16).rearrange("p (i n) -> p i n", i=3)
        dam_rows = work[0:L * H, 1472:1600].bitcast(BF16)
        one_col = sb("one_col", [P, 1])
        eps_col = sb("eps_col", [P, G])
        m1 = sb("m1", [P, 2, UH])
        nm1 = sb("nm1", [P, 2, UH])
        z1 = sb("z1", [P, 2, UH])
        rz1 = sb("rz1", [P, 2, UH])
        m2 = sb("m2", [P, 2, UH])
        nm2 = sb("nm2", [P, 2, UH])
        z2 = sb("z2", [P, 2, UH])
        rz2 = sb("rz2", [P, 2, UH])

        scores_ps = [ctx.enter_context(nc.psum_tensor(f"scores_ps{i}", [P, UW], F32)) for i in range(2)]
        gen_ps = [ctx.enter_context(nc.psum_tensor(f"gen_ps{i}", [P, BANK], F32)) for i in range(GEN_BANKS)]

        weights_in, setup_in, parts_out, toeplitz_in = (
            sem(n) for n in ("weights_in", "setup_in", "parts_out", "toeplitz_in"))
        pool_step, pool_ready, dve_step, gamma_ready, parts_ready, dve_ready, act_step = (
            sem(n) for n in ("pool_step", "pool_ready", "dve_step", "gamma_ready", "parts_ready", "dve_ready",
                             "act_step"))
        iota_ready, pos_ready, masks_ready = (sem(n) for n in ("iota_ready", "pos_ready", "masks_ready"))
        loaded = {n: sem(f"{n}_in") for n in ("ctx_f", "x_f", "cx_f", "ctx_t", "x_t", "pad_mask", "pad_bias")}
        gen_full = [sem(f"gen_full{i}") for i in range(GEN_BANKS)]
        gen_free = [sem(f"gen_free{i}") for i in range(GEN_BANKS)]
        diag_in = [sem(f"diag_in{i}") for i in range(2)]
        xdiag_in = [sem(f"xdiag_in{i}") for i in range(2)]
        scores_done = sem("scores_done")
        scores_free = [sem(f"scores_free{i}") for i in range(2)]
        max1_done, nm1_done, exp1_done, scan_done, recip_done, rz1_done, x_done = (
            sem(n) for n in ("max1_done", "nm1_done", "exp1_done", "scan_done", "recip_done", "rz1_done", "x_done"))
        ln_done, root_done, te_done, select_done, max2_done, nm2_done, exp2_done = (
            sem(n) for n in ("ln_done", "root_done", "te_done", "select_done", "max2_done", "nm2_done", "exp2_done"))
        z2_fixed, rz2_done, norm_done = (sem(n) for n in ("z2_fixed", "rz2_done", "norm_done"))
        stats_done, moments_done, var_done, rstd_done, scaled_done, tok_done = (
            sem(n) for n in ("stats_done", "moments_done", "var_done", "rstd_done", "scaled_done", "tok_done"))
        passed = sem("passed")
        out_done = sem("out_done")
        SETUP_LOADS = 16 * (1 + 2 + ROWS + 1)
        PARTS_OUT = 16 * 7

        def norm_row(l, which):
            return 5 if l == 3 else (l if which == 1 else 3 + FFN_LAYERS.index(l))

        def residual(l, which):
            return a_tok if which == 2 else (ctx_t, x_t, x1_tok, x2_tok)[l]

        def norm_out(l, which):
            if l == 3:
                return out_t
            return (a_tok, x1_tok, a_tok)[l] if which == 1 else (y_tok if l == 0 else x2_tok)

        def values(l):
            return v_t[0 if l == 0 else 1]

        def wait_apart(eng, sem_, value):
            eng.wait_ge(sem_, value)
            eng.sem_inc(passed, 1)

        def read_out(eng, now, d, *steps, back=0, apart=False):
            for i in range(GEN_BANKS):
                order = gen_order[i]
                mine = [step for step in steps if GEN_BANK[step] == i]
                if mine:
                    last = max(mine, key=lambda step: (order.late[step], order.index[step]))
                    eng.wait_ge(gen_free[i], order.upto(now, d, last, back))
                    if apart:
                        eng.sem_inc(passed, 1)

        def take(eng, now, d, step):
            i = GEN_BANK[step]
            eng.wait_ge(gen_full[i], gen_order[i].upto(now, d, step))
            return gen_ps[i], gen_free[i]

        def wait_turned(eng, now, d, u):
            back, (_, last) = bank_order[PARITY[u]].last(("scores", u))
            i = GEN_BANK["pt", last, 1]
            eng.wait_ge(gen_full[i], gen_order[i].upto(now, d, ("pt", last, 1), back))

        def unit_heads(ap):
            return ap.rearrange("p (h k) -> p h k", k=S)

        def read(eng, vector, now, g, d, step):
            if step[0] == "kx":
                eng.wait_ge(loaded["pad_mask"], 16 * (g + 1))
            ps, free = take(eng, now, d, step)
            copy = nc.vector.tensor_copy if vector else nc.scalar.copy
            kind = step[0]
            if kind == "pt":
                _, u, half = step
                last = copy(probs_f[:, PARITY[u], half * BANK:(half + 1) * BANK], ps[:, :])
            elif kind == "att":
                u = step[1]
                if is_layer(u):
                    last = copy(att_f[:, u[1], :, :].rearrange("p c s -> p (c s)"), ps[:, 0:C * S])
                else:
                    last = copy(xatt_f[:, u[1], u[2], :], ps[:, 0:S])
            elif kind == "turn":
                l, which = step[1:]
                dst = h_buf if (l == 1 or (l == 2 and which == 2)) else f_buf
                last = copy(dst[:, :, :].rearrange("p c n -> p (c n)"), ps[:, :])
            elif kind == "k":
                l = step[1]
                for c in range(C):
                    dst, src, bias = k_f[l % 2][:, c, :], ps[:, c * T:(c + 1) * T], k_bias[:, l, c:c + 1]
                    if vector:
                        last = nc.vector.tensor_scalar(dst, src, bias, None, ALU.add)
                    else:
                        last = nc.scalar.activation(dst, src, ACT.Identity, bias=bias)
            elif kind == "v":
                last = copy(values(step[1])[:, :, :].rearrange("p b d -> p (b d)"), ps[:, :])
            elif kind == "kx":
                last = nc.vector.tensor_tensor(xk_f[:, :, :], ps[:, :].rearrange("p (c n) -> p c n", c=C),
                                               pad_mask[:, :].unsqueeze(1).to_broadcast([P, C, T]), ALU.mult)
            elif kind == "vx":
                heads = ps[:, :].rearrange("p (q e d) -> p q e d", e=2, d=XDK)
                for e in range(2):
                    last = copy(xv_t[:, :, :, e, e, :].rearrange("p b q d -> p (b q) d"), heads[:, :, e, :])
            elif kind == "q":
                last = copy(q_f[:, :, :].rearrange("p c n -> p (c n)"), ps[:, :])
            else:
                _, l, pair = step
                for i in range(2):
                    f = 2 * pair + i
                    src, bias = ps[:, i * T:(i + 1) * T], up_bias[:, FFN_LAYERS.index(l), f:f + 1]
                    if vector:
                        last = nc.vector.tensor_scalar(hidden[:, f, :], src, bias, 0.0, ALU.add, ALU.max)
                    else:
                        last = nc.scalar.activation(hidden[:, f, :], src, ACT.Relu, bias=bias)
            last.then_inc(free, 1)

        block = ctx.enter_context(nc.Block())

        @block.sync
        def _(sp):
            sp.dma_start(gam[:, 0, :], bass.AP(t["gammas"].tensor, 0, [[0, P], [1, L * H]])).then_inc(setup_in, 16)
            sp.dma_start(logits[:, :, :], t["alphas"].rearrange("l h s e -> (l h) s e")).then_inc(setup_in, 16)
            sp.dma_start(gumbel[:, :, :], t["gumbel"].rearrange("l h s e -> (l h) s e")).then_inc(setup_in, 16)
            for i, src in enumerate([t["vb"][0], t["vb"][1], t["vb"][2], t["ob"][0], t["ob"][1], t["ob"][2],
                                     t["b2"][0], t["b2"][2], t["bo"]]):
                sp.dma_start(rows[i:i + 1, :], src.unsqueeze(0)).then_inc(setup_in, 16)
            sp.dma_start(pads[:, :], t["pad"]).then_inc(setup_in, 16)
            n_w = 0
            for l in range(L):
                for dst, name in ((k_w, "kWT"), (v_w, "vWT"), (o_w, "oWT")):
                    sp.dma_start(dst[l][:, :, :], t[name][l].rearrange("(c p) n -> p c n", p=P)).then_inc(weights_in, 16)
                n_w += 3
            sp.dma_start(k_bias[:, :, :], t["kb"]).then_inc(weights_in, 16)
            sp.dma_start(up_bias[:, :, :], t["b1"]).then_inc(weights_in, 16)
            n_w += 2
            for i, l in enumerate(FFN_LAYERS):
                sp.dma_start(up_w[l][:, :, :], t["w1T"][l].rearrange("(c p) n -> p c n", p=P)).then_inc(weights_in, 16)
                sp.dma_start(down_w[l][:, :, :], t["w2T"][l].rearrange("(c p) n -> p c n", p=P)).then_inc(weights_in, 16)
                n_w += 2
            for dst, name in ((xq_w, "wq"), (xk_w, "wk"), (xv_w, "wv"), (xo_w, "wo")):
                sp.dma_start(dst[:, :, :], t[name].rearrange("(c p) n -> p c n", p=P)).then_inc(weights_in, 16)
                n_w += 1

            sp.wait_ge(parts_ready, 3)
            for i in range(3):
                sp.dma_start(row_bias[i:i + 1, :, :], rows_parts[:, i, :]).then_inc(parts_out, 16)
                sp.dma_start(pad_parts_dram[i].rearrange("(b s) -> b s", b=B), pads_parts[:, i, :]).then_inc(parts_out, 16)
            sp.dma_start(dam_rows_dram, dam_rows[:, :].unsqueeze(1).to_broadcast([L * H, P, 2 * S])).then_inc(parts_out, 16)
            sp.wait_ge(parts_out, PARTS_OUT)
            for l in range(L):
                src = bass.AP(dam_rows_dram.tensor, l * H * P * 2 * S + S, [[2 * S - 1, P], [P * 2 * S, H], [1, S]])
                sp.dma_start(dam_bias[l][:, :, :], src).then_inc(toeplitz_in, 16)
            for dst, srcs in ((norm_g, [t["ln1_g"][0], t["ln1_g"][1], t["ln1_g"][2], t["ln2_g"][0], t["ln2_g"][2],
                                        t["ln_gamma"]]),
                              (norm_b, [t["ln1_b"][0], t["ln1_b"][1], t["ln1_b"][2], t["ln2_b"][0], t["ln2_b"][2],
                                        t["ln_beta"]])):
                for i, src in enumerate(srcs):
                    sp.dma_start(dst[:, i, :], bass.AP(src.tensor, src.offset, [[0, P], [1, D]])).then_inc(weights_in, 16)
                    n_w += 1
            assert n_w == N_WEIGHTS
            sp.wait_ge(masks_ready, 2)

            def diag_blocks(now, d, u):
                b, slot = u[1], PARITY[u]
                read_out(sp, now, d, ("k", u[0]) if is_layer(u) else ("kx",), apart=True)
                order = (diag_order if is_layer(u) else xdiag_order)[slot]
                back, (_, last) = order.last(("diag", u))
                wait_apart(sp, scores_done, scores_order.upto(now, d, ("scores", last), back))
                if is_layer(u):
                    for c in range(C):
                        for j in range(P // DK):
                            rows_j = slice(j * DK, (j + 1) * DK)
                            col = c * BANK + j * S
                            sp.dma_start(k_diag[rows_j, slot, col:col + S],
                                         k_f[u[0] % 2][rows_j, c, b * S:(b + 1) * S]).then_inc(diag_in[slot], 16)
                else:
                    for j in range(UH):
                        rows_j = slice(j * XDK, (j + 1) * XDK)
                        sp.dma_start(xk_diag[rows_j, slot, j * S:(j + 1) * S],
                                     xk_f[rows_j, u[2], b * S:(b + 1) * S]).then_inc(xdiag_in[slot], 16)

            def load(now, g, d, name):
                tok = bass.ds(g * T, T)
                done = loaded[name]
                if name in ("ctx_f", "x_f", "cx_f"):
                    dst, src, readers = {
                        "ctx_f": (ctx_f, "ctxT", [("k", 0), ("v", 0)]), "x_f": (x_f, "xT", [("k", 1), ("v", 1)]),
                        "cx_f": (cx_f, "ctxT", [("kx",), ("vx",)])}[name]
                    read_out(sp, now, d, *readers, back=1, apart=True)
                    sp.dma_start(dst[:, :, :], t[src][:, tok].rearrange("(c p) n -> p c n", p=P)).then_inc(done, 16)
                elif name in ("ctx_t", "x_t"):
                    dst, src, l = (ctx_t, "ctx", 0) if name == "ctx_t" else (x_t, "x", 1)
                    read_out(sp, now, d, ("o", l), back=1, apart=True)
                    sp.dma_start(dst[:, :, :], t[src][tok, :].rearrange("(b s) d -> s b d", s=S)).then_inc(done, 16)
                elif name == "pad_mask":
                    read_out(sp, now, d, ("kx",), back=1, apart=True)
                    sp.dma_start(pad_mask[:, :], bass.AP(t["pad"].tensor, g * T, [[0, P], [1, T]])).then_inc(done, 16)
                else:
                    _, last = max((scores_order.late[step] * len(PARITY) + i, step)
                                     for i, (_, step) in enumerate(scores_order.events) if not layer_step(step))
                    wait_apart(sp, scores_done, scores_order.upto(now, d, last, 1))
                    sp.dma_start(pad_bias[:, :], pad_parts_dram[:, tok]).then_inc(done, 16)

            def store(now, g, d):
                wait_apart(sp, tok_done, tok_order.upto(now, d, ("tok", 3, 1)))
                sp.dma_start(t["out"][bass.ds(g * T, T), :].rearrange("(b s) d -> s b d", s=S), out_t[:, :, :]
                             ).then_inc(out_done, 16)

            def turn_of(now):
                for g, d, step in now.steps(SYNC):
                    if step[0] == "diag":
                        diag_blocks(now, d, step[1])
                    elif step[0] == "load":
                        load(now, g, d, step[1])
                    else:
                        store(now, g, d)

            run_turns(sp, turn_of)
            sp.wait_ge(out_done, 16 * GROUPS + SEED)

        @block.tensor
        def _(pe):
            pe.wait_ge(weights_in, 16 * N_WEIGHTS)
            pe.wait_ge(parts_out, PARTS_OUT)
            pe.wait_ge(dve_ready, 1)
            pe.wait_ge(masks_ready, 2)
            pe.wait_ge(pool_ready, 1)

            def in_sbuf(now, d, step, *needs):
                read_out(pe, now, d, *[need for need in needs if GEN_BANK[need] != GEN_BANK[step]])

            def add_row(out, row):
                return nc.tensor.matmul(out, ones3[:, :], row_bias[:, row, :], start=False, stop=True)

            def feature_major(ps, w, src, chunks):
                for i, c in enumerate(chunks):
                    for k in range(C):
                        mm = nc.tensor.matmul(ps[:, i * T:(i + 1) * T], w[:, k, c * P:(c + 1) * P], src[:, k, :],
                                              start=(k == 0), stop=(k == C - 1))
                return mm

            def token_major(ps, w, src, row):
                for b in range(G):
                    out = ps[:, b * D:(b + 1) * D]
                    for k in range(C):
                        mm = nc.tensor.matmul(out, src[:, k, b * S:(b + 1) * S], w[:, k, :], start=(k == 0),
                                              stop=(k == C - 1 and row is None))
                    if row is not None:
                        mm = add_row(out, row)
                return mm

            def scores(now, g, d, u):
                p, b = PARITY[u], u[1]
                out = scores_ps[p]
                pe.wait_ge(scores_free[p], bank_order[p].before(now, d, ("scores", u)))
                if is_layer(u):
                    l = u[0]
                    pe.wait_ge(diag_in[p], (diag_order[p].upto(now, d, ("diag", u)) - SEED) * 16 * UH)
                    for c in range(C):
                        half = slice(c * BANK, (c + 1) * BANK)
                        nc.tensor.matmul(out[:, half], k_f[l % 2][:, c, b * S:(b + 1) * S], k_diag[:, p, half],
                                         start=True, stop=False)
                        mm = nc.tensor.matmul(out[:, half], ident_bf[:, :],
                                              dam_bias[l][:, c * 4:(c + 1) * 4, :].rearrange("p h k -> p (h k)"),
                                              start=False, stop=True)
                else:
                    pe.wait_ge(xdiag_in[p], (xdiag_order[p].upto(now, d, ("diag", u)) - SEED) * 16 * UH)
                    pe.wait_ge(loaded["pad_bias"], 16 * (g + 1))
                    read_out(pe, now, d, ("q",))
                    for half in range(2):
                        cols = slice(half * BANK, (half + 1) * BANK)
                        nc.tensor.matmul(out[:, cols], q_f[:, u[2], b * S:(b + 1) * S], xk_diag[:, p, cols],
                                         start=True, stop=False)
                        bias = pad_bias[:, b * S:(b + 1) * S].unsqueeze(1).to_broadcast([3, BANK // S, S])
                        mm = nc.tensor.matmul(out[:, cols], ones3[:, :], bias, start=False, stop=True)
                mm.then_inc(scores_done, 1)

            def probs_turn(ps, now, d, u, half):
                pe.wait_ge(norm_done, prob_order.upto(now, d, ("prob", u)))
                for j in range(4):
                    h = half * 4 + j
                    mm = nc.tensor.transpose(ps[:, j * S:(j + 1) * S], X[:, PARITY[u], h * S:(h + 1) * S], ident[:, :])
                return mm

            def attend(ps, now, d, u):
                b = u[1]
                value_step = ("v", u[0]) if is_layer(u) else ("vx",)
                for half in range(2):
                    in_sbuf(now, d, ("att", u), ("pt", u, half), *([value_step] if half == 0 else []))
                    for j in range(4):
                        h = half * 4 + j
                        probs = probs_f[:, PARITY[u], h * S:(h + 1) * S]
                        if is_layer(u):
                            mm = nc.tensor.matmul(ps[j * DK:(j + 1) * DK, half * S:(half + 1) * S],
                                                  values(u[0])[:, b, h * DK:(h + 1) * DK], probs, start=True, stop=True)
                        else:
                            pair, e = h // 2, h % 2
                            v = xv_t[:, b, u[2] * 4 + pair, e, :, :].rearrange("p e d -> p (e d)")
                            mm = nc.tensor.matmul(ps[pair * 32:(pair + 1) * 32, 0:S], v, probs,
                                                  start=(e == 0), stop=(e == 1))
                return mm

            def out_proj(ps, now, d, l):
                in_sbuf(now, d, ("o", l), *[("att", u) for u in PARITY if u[0] == l])
                w, att, row = (o_w[l], att_f, 3 + l) if l < L else (xo_w, xatt_f, 8)
                for b in range(G):
                    out = ps[:, b * D:(b + 1) * D]
                    for c in range(C):
                        nc.tensor.matmul(out, att[:, b, c, :], w[:, c, :], start=(c == 0), stop=False)
                    mm = add_row(out, row)
                return mm

            def turn(ps, now, d, l, which):
                pe.wait_ge(tok_done, tok_order.upto(now, d, ("tok", l, which)))
                for c in range(C):
                    for b in range(G):
                        mm = nc.tensor.transpose(ps[:, (c * G + b) * S:(c * G + b + 1) * S],
                                                 norm_out(l, which)[:, b, c * P:(c + 1) * P], ident[:, :])
                return mm

            def project(ps, now, g, d, step):
                kind = step[0]
                if kind in ("k", "v") and step[1] < 2:
                    pe.wait_ge(loaded[("ctx_f", "x_f")[step[1]]], 16 * (g + 1))
                if kind in ("kx", "vx"):
                    pe.wait_ge(loaded["cx_f"], 16 * (g + 1))
                if kind == "k":
                    l = step[1]
                    if l == 2:
                        in_sbuf(now, d, step, ("turn", 1, 1))
                    return feature_major(ps, k_w[l], (ctx_f, x_f, h_buf)[l], range(C))
                if kind == "v":
                    l = step[1]
                    if l == 2:
                        in_sbuf(now, d, step, ("turn", 0, 2))
                    return token_major(ps, v_w[l], (ctx_f, x_f, f_buf)[l], l)
                if kind == "kx":
                    return feature_major(ps, xk_w, cx_f, range(C))
                if kind == "vx":
                    return token_major(ps, xv_w, cx_f, None)
                in_sbuf(now, d, step, ("turn", 2, 2))
                return feature_major(ps, xq_w, h_buf, range(C))

            def up(ps, now, d, l, pair):
                in_sbuf(now, d, ("up", l, pair), ("turn", l, 1))
                return feature_major(ps, up_w[l], f_buf, (2 * pair, 2 * pair + 1))

            def down(ps, now, d, l):
                for b in range(G):
                    out = ps[:, b * D:(b + 1) * D]
                    for f in range(FC):
                        if b == 0 and f % 2 == 0:
                            in_sbuf(now, d, ("down", l), ("up", l, f // 2))
                        nc.tensor.matmul(out, hidden[:, f, b * S:(b + 1) * S], down_w[l][:, f, :],
                                         start=(f == 0), stop=False)
                    mm = add_row(out, 6 + FFN_LAYERS.index(l))
                return mm

            def turn_of(now):
                for g, d, step in now.steps(TENSOR):
                    if step[0] == "scores":
                        scores(now, g, d, step[1])
                        continue
                    i = GEN_BANK[step]
                    pe.wait_ge(gen_free[i], gen_order[i].before(now, d, step))
                    ps = gen_ps[i]
                    if step[0] == "pt":
                        last = probs_turn(ps, now, d, *step[1:])
                    elif step[0] == "att":
                        last = attend(ps, now, d, step[1])
                    elif step[0] == "o":
                        last = out_proj(ps, now, d, step[1])
                    elif step[0] == "turn":
                        last = turn(ps, now, d, *step[1:])
                    elif step[0] == "up":
                        last = up(ps, now, d, *step[1:])
                    elif step[0] == "down":
                        last = down(ps, now, d, *step[1:])
                    else:
                        last = project(ps, now, g, d, step)
                    last.then_inc(gen_full[i], 1)

            run_turns(pe, turn_of)

        @block.scalar
        def _(act):
            nc.scalar.preload_act_table_set("natural_log_exp_and_others")
            act.wait_ge(pool_ready, 1)
            act.wait_ge(gamma_ready, 1)
            nc.scalar.activation(gam[:, 1, :], gam[:, 1, :], ACT.Exp, scale=-1.0).then_inc(act_step, 1)
            act.wait_ge(act_step, 1)
            nc.scalar.activation(gam[:, 1, :], gam[:, 1, :], ACT.Ln, bias=one_col[:, :]).then_inc(act_step, 1)
            nc.scalar.activation(gumbel[:, :, :], gumbel[:, :, :], ACT.Ln, bias=eps_col[0:L * H, 0:1]).then_inc(act_step, 1)
            act.wait_ge(weights_in, 16 * N_WEIGHTS)
            act.wait_ge(dve_ready, 1)

            def exps(src, minus_max, dst, sums, scale, done):
                for h in range(UH):
                    cols = slice(h * S, (h + 1) * S)
                    a = nc.scalar.activation(dst[:, cols], src[:, cols], ACT.Exp, bias=minus_max[:, h:h + 1], scale=scale,
                                             accum_out=sums[:, h:h + 1])
                a.then_inc(done, 1)

            def scanned(now, d, u):
                back, (_, last) = exp1_order.last(("exp1", u))
                return dist_order.upto(now, d, ("dist", last), back)

            def exp1(now, d, u):
                p = PARITY[u]
                act.wait_ge(nm1_done, neg1_order.upto(now, d, ("neg1", u)))
                if is_layer(u):
                    act.wait_ge(scan_done, scanned(now, d, u))
                    exps(scores_ps[p], nm1[:, p, :], E[:, :], z1[:, p, :], SCALE, exp1_done)
                else:
                    wait_turned(act, now, d, u)
                    exps(scores_ps[p], nm1[:, p, :], X[:, p, :], z2[:, p, :], XSCALE, scores_free[p])

            def effect(now, d, u):
                n = effect_order.upto(now, d, ("effect", u))
                x = X[:, PARITY[u], :]
                act.wait_ge(x_done, dist_order.upto(now, d, ("dist", u)))
                nc.scalar.activation(x, x, ACT.Ln, bias=root_floor[:, :]).then_inc(ln_done, 1)
                act.wait_ge(ln_done, n)
                nc.scalar.activation(x, x, ACT.Exp, scale=0.5).then_inc(root_done, 1)
                act.wait_ge(root_done, n)
                nc.scalar.activation(x, x, ACT.Exp, scale=-1.0).then_inc(te_done, 1)

            def exp2(now, d, u):
                p = PARITY[u]
                act.wait_ge(nm2_done, neg2_order.upto(now, d, ("neg2", u)))
                exps(X[:, p, :], nm2[:, p, :], X[:, p, :], z2[:, p, :], SCALE, exp2_done)

            def turn_of(now):
                for g, d, step in now.steps(SCALAR):
                    if step[0] in GENERAL_KINDS:
                        read(act, False, now, g, d, step)
                    else:
                        {"exp1": exp1, "effect": effect, "exp2": exp2}[step[0]](now, d, step[1])

            run_turns(act, turn_of)

        @block.vector
        def _(dve):
            steps = [0]

            def link(ins):
                steps[0] += 1
                ins.then_inc(dve_step, 1)
                dve.wait_ge(dve_step, steps[0])

            dve.wait_ge(setup_in, SETUP_LOADS)
            link(nc.vector.tensor_scalar(gam[:, 3, :], gam[:, 0, :], -1.0, None, ALU.mult))
            link(nc.vector.tensor_scalar(gam[:, 2, :], gam[:, 0, :], 0.0, None, ALU.max))
            nc.vector.tensor_tensor(gam[:, 1, :], gam[:, 0, :], gam[:, 3, :], ALU.max).then_inc(gamma_ready, 1)
            link(nc.vector.tensor_scalar(pads[:, :], pads[:, :], -1.0, PAD_BIAS, ALU.add, ALU.mult))
            for whole, parts in ((pads, pads_parts), (rows, rows_parts)):
                for i in range(3):
                    ins = nc.vector.tensor_copy(parts[:, i, :], whole[:, :])
                    if i < 2:
                        link(ins)
                        link(nc.vector.tensor_tensor(whole[:, :], whole[:, :], parts[:, i, :], ALU.subtract))
                    else:
                        ins.then_inc(parts_ready, 1)
            dve.wait_ge(act_step, 3)
            link(nc.vector.tensor_tensor(logits[:, :, :], logits[:, :, :], gumbel[:, :, :], ALU.subtract))
            link(nc.vector.tensor_tensor(gumbel[:, :, 0], logits[:, :, 0], logits[:, :, 1], ALU.is_ge))
            link(nc.vector.memset(dam_rows[:, 0:S], 0.0))
            link(nc.vector.tensor_scalar(dam_rows[:, S:2 * S], gumbel[:, :, 0], MASKED, None, ALU.mult))
            nc.vector.memset(dam_rows[0:2 * H, S:S + 1], 0.0).then_inc(parts_ready, 1)
            link(nc.vector.tensor_tensor(gam[:, 1, :], gam[:, 1, :], gam[:, 2, :], ALU.add))
            link(nc.vector.tensor_tensor(gam[:, 1, :], gam[:, 1, :], gam[:, 1, :], ALU.mult))
            dve.wait_ge(iota_ready, 1)
            nc.vector.tensor_copy(pos_f[:, 2, :], iota_i[:, :]).then_inc(pos_ready, 1)
            dve.wait_ge(masks_ready, 1)
            for m in (0, 1):
                for h in range(UH):
                    link(nc.vector.tensor_scalar(chain[m][:, h * S:(h + 1) * S], pos_f[:, m, :], 0.0, None, ALU.is_gt))
            link(nc.vector.tensor_copy(ident_bf[:, :], ident[:, :]))
            dve.wait_ge(toeplitz_in, 16 * L)
            nc.vector.memset(dam_bias[2][0:1, :, 0:1], 0.0).then_inc(dve_ready, 1)
            dve.wait_ge(weights_in, 16 * N_WEIGHTS)
            dve.wait_ge(pool_ready, 1)

            def max1(now, d, u):
                p = PARITY[u]
                dve.wait_ge(scores_done, scores_order.upto(now, d, ("scores", u)))
                nc.vector.tensor_reduce(m1[:, p, :], unit_heads(scores_ps[p][:, :]), AX_X, ALU.max).then_inc(max1_done, 1)

            def neg1(now, d, u):
                p = PARITY[u]
                dve.wait_ge(max1_done, max1_order.upto(now, d, ("max1", u)))
                nc.vector.tensor_scalar(nm1[:, p, :], m1[:, p, :], -(SCALE if is_layer(u) else XSCALE), None, ALU.mult
                                        ).then_inc(nm1_done, 1)

            def distance(now, d, u):
                p, l, n = PARITY[u], u[0], dist_order.upto(now, d, ("dist", u))
                dve.wait_ge(exp1_done, exp1_order.upto(now, d, ("exp1", u)))
                nc.vector.reciprocal(rz1[:, p, :], z1[:, p, :]).then_inc(recip_done, 1)
                dve.wait_ge(x_done, dist_order.before(now, d, ("dist", u)))
                nc.vector.tensor_tensor_scan(suffix[:, UW - 1::-1], chain[FIRST_KEY_MASK[l]][:, ::-1], E[:, ::-1], 0.0,
                                             ALU.mult, ALU.add).then_inc(scan_done, 1)
                dve.wait_ge(recip_done, n)
                nc.vector.tensor_tensor(rz1[:, p, :], rz1[:, p, :], gam[:, 1, l * H:(l + 1) * H], ALU.mult
                                        ).then_inc(rz1_done, 1)
                dve.wait_ge(rz1_done, n)
                dve.wait_ge(scan_done, n)
                wait_turned(dve, now, d, u)
                for h in range(UH):
                    ins = nc.vector.scalar_tensor_tensor(out=X[:, p, h * S:(h + 1) * S],
                                                         in0=suffix[:, h * S + 1:(h + 1) * S + 1],
                                                         scalar=rz1[:, p, h:h + 1], in1=pos_f[:, FIRST_KEY_MASK[l], :],
                                                         op0=ALU.mult, op1=ALU.mult)
                ins.then_inc(x_done, 1)

            def scores2(now, d, u):
                p = PARITY[u]
                dve.wait_ge(te_done, effect_order.upto(now, d, ("effect", u)))
                nc.vector.scalar_tensor_tensor(out=X[:, p, :], in0=X[:, p, :], scalar=1e-5, in1=scores_ps[p][:, :],
                                               op0=ALU.max, op1=ALU.mult).then_inc(scores_free[p], 1)

            def max2(now, d, u):
                p = PARITY[u]
                dve.wait_ge(select_done, select_order.upto(now, d, ("select", u)))
                nc.vector.tensor_reduce(m2[:, p, :], unit_heads(X[:, p, :]), AX_X, ALU.max).then_inc(max2_done, 1)

            def neg2(now, d, u):
                p = PARITY[u]
                dve.wait_ge(max2_done, max2_order.upto(now, d, ("max2", u)))
                keep = keep_row[:, 0:1] if u[0] == 2 else 1.0
                nc.vector.tensor_scalar(nm2[:, p, :], m2[:, p, :], -SCALE, keep, ALU.mult, ALU.mult
                                        ).then_inc(nm2_done, 1)

            def recip(now, d, u):
                p = PARITY[u]
                if is_layer(u):
                    dve.wait_ge(exp2_done, exp2_order.upto(now, d, ("exp2", u)))
                else:
                    dve.wait_ge(scores_free[p], bank_order[p].upto(now, d, ("scores", u)))
                if u[0] == 2:
                    nc.vector.tensor_scalar(z2[:, p, :], z2[:, p, :], first_row[:, 0:1], None, ALU.add
                                            ).then_inc(z2_fixed, 1)
                    dve.wait_ge(z2_fixed, fixed_order.upto(now, d, ("recip", u)))
                nc.vector.reciprocal(rz2[:, p, :], z2[:, p, :]).then_inc(rz2_done, 1)

            def normalise(now, d, u):
                p = PARITY[u]
                dve.wait_ge(rz2_done, recip_order.upto(now, d, ("recip", u)))
                nc.vector.tensor_tensor(unit_heads(X[:, p, :]), unit_heads(X[:, p, :]),
                                        rz2[:, p, :].unsqueeze(2).to_broadcast([P, UH, S]), ALU.mult
                                        ).then_inc(norm_done, 1)

            def norm_sums(now, g, d, l, which):
                key = ("sums", l, which)
                i, n = NORM_SLOT[l, which], sums_order.upto(now, d, key)
                step = ("o", l) if which == 1 else ("down", l)
                back, last = sums_order.last(key, 2)
                dve.wait_ge(tok_done, tok_order.upto(now, d, ("tok",) + last[1:], back))
                ps, free = take(dve, now, d, step)
                if which == 1 and l < 2:
                    dve.wait_ge(loaded[("ctx_t", "x_t")[l]], 16 * (g + 1))
                nc.vector.tensor_tensor(res[:, i, :, :], ps[:, :].rearrange("p (b d) -> p b d", b=G),
                                        residual(l, which)[:, :, :], ALU.add).then_inc(free, 1)
                read_out(dve, now, d, step)
                for b in range(G):
                    ins = nc.vector.bn_stats(stats[:, i, b, :], res[:, i, b, :])
                ins.then_inc(stats_done, 1)
                wait_apart(dve, stats_done, n)
                for b in range(G):
                    ins = nc.vector.bn_aggr(moments[:, i, b, :], stats[:, i, b, :])
                ins.then_inc(moments_done, 1)
                dve.wait_ge(moments_done, n)
                for b in range(G):
                    ins = nc.vector.scalar_tensor_tensor(out=res[:, i, b, :], in0=res[:, i, b, :],
                                                         scalar=moments[:, i, b, 0:1],
                                                         in1=norm_g[:, norm_row(l, which), :],
                                                         op0=ALU.subtract, op1=ALU.mult)
                ins.then_inc(scaled_done, 1)

            def norm_tokens(now, g, d, l, which):
                i = NORM_SLOT[l, which]
                dve.wait_ge(scaled_done, sums_order.upto(now, d, ("sums", l, which)))
                dve.wait_ge(rstd_done, dev_order.upto(now, d, ("dev", l, which)))
                if l == 3:
                    dve.wait_ge(out_done, 16 * g + SEED)
                for b in range(G):
                    ins = nc.vector.scalar_tensor_tensor(out=norm_out(l, which)[:, b, :], in0=res[:, i, b, :],
                                                         scalar=rstd[:, i, b:b + 1],
                                                         in1=norm_b[:, norm_row(l, which), :], op0=ALU.mult, op1=ALU.add)
                ins.then_inc(tok_done, 1)

            def turn_of(now):
                for g, d, step in now.steps(VECTOR):
                    if step[0] in GENERAL_KINDS:
                        read(dve, True, now, g, d, step)
                    elif step[0] == "sums":
                        norm_sums(now, g, d, *step[1:])
                    elif step[0] == "tok":
                        norm_tokens(now, g, d, *step[1:])
                    else:
                        {"max1": max1, "neg1": neg1, "dist": distance, "scores2": scores2, "max2": max2, "neg2": neg2,
                         "recip": recip, "prob": normalise}[step[0]](now, d, step[1])

            run_turns(dve, turn_of)

        @block.gpsimd
        def _(pool):
            n_pool = [0]

            def link(ins):
                n_pool[0] += 1
                ins.then_inc(pool_step, 1)
                pool.wait_ge(pool_step, n_pool[0])

            for seeded in (*gen_free, *gen_full, *scores_free, z2_fixed, out_done, scores_done, max1_done, nm1_done,
                           exp1_done, scan_done, recip_done, rz1_done, x_done, ln_done, root_done, te_done, select_done,
                           max2_done, nm2_done, exp2_done, rz2_done, norm_done, stats_done, moments_done, var_done,
                           rstd_done, scaled_done, tok_done):
                pool.sem_inc(seeded, SEED)
            nc.gpsimd.iota(iota_i[:, :], [[-1, S]], base=0, channel_multiplier=1).then_inc(iota_ready, 1)
            for tile, value in ((root_floor, ROOT_FLOOR), (neg_half, -0.5), (one_col, 1.0), (eps_col, 1e-5),
                                (keep_row, 1.0), (first_row, 0.0), (ident, 0.0), (ones3, 1.0)):
                link(nc.gpsimd.memset(tile[:, :], value))
            link(nc.gpsimd.memset(keep_row[0:1, :], 0.0))
            link(nc.gpsimd.memset(first_row[0:1, :], 1.0))
            link(nc.gpsimd.memset(suffix[:, UW:UW + 1], 0.0))
            link(nc.gpsimd.affine_select(out=ident[:, :], in_=ident[:, :], compare_op=ALU.not_equal, fill=1.0, base=0,
                                         pattern=[[-1, P]], channel_multiplier=1))
            nc.gpsimd.memset(xv_t[:, :, :, :, :, :], 0.0).then_inc(pool_ready, 1)
            pool.wait_ge(pos_ready, 1)
            for m in (0, 1):
                ins = nc.gpsimd.affine_select(out=pos_f[:, m, :], in_=pos_f[:, 2, :], compare_op=ALU.is_gt, fill=0.0,
                                              base=m - 1, pattern=[[-1, S]], channel_multiplier=1)
                if m == 0:
                    link(ins)
            ins.then_inc(masks_ready, 1)
            link(nc.gpsimd.memset(k_diag[:, :, :], 0.0))
            nc.gpsimd.memset(xk_diag[:, :, :], 0.0).then_inc(masks_ready, 1)

            def select(now, d, u):
                p, m = PARITY[u], FIRST_KEY_MASK[u[0]]
                wait_apart(pool, scores_free[p], bank_order[p].upto(now, d, ("scores", u)))
                x = unit_heads(X[:, p, :])
                nc.gpsimd.affine_select(out=x, in_=x, compare_op=ALU.is_gt, fill=MASKED, base=m,
                                        pattern=[[0, UH], [-1, S]], channel_multiplier=1).then_inc(select_done, 1)

            def deviation(now, d, l, which):
                i, n = NORM_SLOT[l, which], dev_order.upto(now, d, ("dev", l, which))
                pool.wait_ge(moments_done, sums_order.upto(now, d, ("sums", l, which)))
                nc.gpsimd.tensor_tensor(rstd[:, i, :], moments[:, i, :, 1], eps_col[:, :], ALU.add).then_inc(var_done, 1)
                pool.wait_ge(var_done, n)
                nc.gpsimd.tensor_tensor(rstd[:, i, :], rstd[:, i, :], neg_half[:, :], ALU.pow).then_inc(rstd_done, 1)

            def turn_of(now):
                for g, d, step in now.steps(POOL):
                    {"select": select, "dev": deviation}[step[0]](now, d, *step[1:])

            run_turns(pool, turn_of)


N_WEIGHTS = 3 * L + 2 + 2 * len(FFN_LAYERS) + 4 + 12


def kernel(x, ctx_1024, mask_BxS2_ff1, L0_xattn_kW, L0_xattn_kb, L0_xattn_vW, L0_xattn_vb, L0_xattn_oW, L0_xattn_ob,
           L0_xattn_gammas, L0_xattn_alphas, L0_xattn_ln1_g, L0_xattn_ln1_b, L0_xattn_w1, L0_xattn_b1, L0_xattn_w2,
           L0_xattn_b2, L0_xattn_ln2_g, L0_xattn_ln2_b, L0_xattn_gumbel_E, L1_xattn_wq, L1_xattn_wk, L1_xattn_wv,
           L1_xattn_wo, L1_xattn_bo, L1_xattn_ln_gamma, L1_xattn_ln_beta):
    import numpy as np
    import concourse.bacc as bacc
    from concourse.bass_utils import run_bass_kernel_spmd

    arr = np.ascontiguousarray
    x, c = np.asarray(x), np.asarray(ctx_1024)
    data = {
        "x": arr(x.reshape(B * S, D)), "ctx": arr(c.reshape(B * S, D)),
        "xT": arr(x.reshape(B * S, D).T), "ctxT": arr(c.reshape(B * S, D).T),
        "pad": arr(np.asarray(mask_BxS2_ff1)),
        "kWT": arr(np.asarray(L0_xattn_kW).transpose(0, 2, 1)), "vWT": arr(np.asarray(L0_xattn_vW).transpose(0, 2, 1)),
        "oWT": arr(np.asarray(L0_xattn_oW).transpose(0, 2, 1)), "w1T": arr(np.asarray(L0_xattn_w1).transpose(0, 2, 1)),
        "w2T": arr(np.asarray(L0_xattn_w2).transpose(0, 2, 1)),
        "kb": arr(np.asarray(L0_xattn_kb).reshape(L, C, P).transpose(2, 0, 1)),
        "b1": arr(np.asarray(L0_xattn_b1)[FFN_LAYERS].reshape(2, FC, P).transpose(2, 0, 1)),
        "vb": L0_xattn_vb, "ob": L0_xattn_ob, "b2": L0_xattn_b2,
        "gammas": L0_xattn_gammas, "alphas": L0_xattn_alphas, "gumbel": L0_xattn_gumbel_E,
        "ln1_g": L0_xattn_ln1_g, "ln1_b": L0_xattn_ln1_b, "ln2_g": L0_xattn_ln2_g, "ln2_b": L0_xattn_ln2_b,
        "wq": L1_xattn_wq, "wk": L1_xattn_wk, "wv": L1_xattn_wv, "wo": L1_xattn_wo, "bo": L1_xattn_bo,
        "ln_gamma": L1_xattn_ln_gamma, "ln_beta": L1_xattn_ln_beta,
    }
    data = {f"in_{n}": arr(a) for n, a in data.items()}
    nc = bacc.Bacc("TRN2", target_bir_lowering=False, num_devices=1)
    t = {n[3:]: nc.dram_tensor(n, a.shape, mybir.dt.from_np(a.dtype), kind="ExternalInput").ap()
         for n, a in data.items()}
    t["out"] = nc.dram_tensor("out", (B * S, D), F32, kind="ExternalOutput").ap()
    build(nc, t)
    r = run_bass_kernel_spmd(nc, [data], core_ids=[0])
    return r.results[0]["out"].reshape(B, S, D)
```
